# Optimizing a Trainium2 kernel written in Bass

```python
import numpy as np
import jax
import jax.numpy as jnp

def _softmax(x, axis=-1):
    return jax.nn.softmax(x, axis=axis)

def _gelu(x):
    return jax.nn.gelu(x, approximate=True)

def _silu(x):
    return jax.nn.silu(x)

def _sigmoid(x):
    return jax.nn.sigmoid(x)

def _layernorm(x, axis=-1, eps=1e-05):
    m = jnp.mean(x, axis=axis, keepdims=True)
    v = jnp.var(x, axis=axis, keepdims=True)
    return (x - m) / jnp.sqrt(v + eps)

def _scatter_add(tgt, idx, src, axis=0):
    return tgt.at[idx].add(src)

def _segment_sum(src, seg, n):
    return jax.ops.segment_sum(src, seg, n)
kernel_name = 'mk_hybrid_d1_jaxref_r8_d96b87'

def setup_inputs(seed: int=0):
    np.random.seed(seed)
    _w = jnp.asarray

    def _L0_attn_a_setup():
        import jax, jax.numpy as jnp
        import numpy as np
        B, N, D = (8, 256, 128)
        A_STDP, TAU_STDP, W_OFF, T_MAX = (0.9, 0.5, 0.9, 1.0)
        V_TH, EPS = (1.0, 1e-05)

        def _proj(x, W, g, b, m, v):
            h = x @ W
            h = (h - m) * (g * jax.lax.rsqrt(v + EPS)) + b
            return jax.nn.sigmoid(4.0 * (h - V_TH))
        key = jax.random.key(seed)
        ks = jax.random.split(key, 6)
        s = 0.02
        inp = {'x': jax.random.normal(ks[0], (B, N, D), dtype=jnp.float32)}
        for i, nm in enumerate(['q', 'k', 'v']):
            inp[f'W{nm}'] = jax.random.normal(ks[1 + i], (D, D), dtype=jnp.float32) * s
            inp[f'g{nm}'] = jnp.ones((D,), jnp.float32)
            inp[f'b{nm}'] = jnp.zeros((D,), jnp.float32)
            inp[f'm{nm}'] = jnp.zeros((D,), jnp.float32)
            inp[f'v{nm}'] = jnp.ones((D,), jnp.float32)
        inp['Wo'] = jax.random.normal(ks[4], (D, D), dtype=jnp.float32) * s
        inp['bo'] = jnp.zeros((D,), jnp.float32)
        return inp
    _L0_attn_a_in = _L0_attn_a_setup()

    def _L0_attn_b_setup():
        import jax, jax.numpy as jnp
        import numpy as np
        B, S, D, H, A = (2, 256, 128, 16, 64)
        INIT_STD = 0.02
        key = jax.random.key(seed)
        ks = jax.random.split(key, 5)
        return {'residual': jax.random.normal(ks[0], (B, S, D), dtype=jnp.float32), 'Wq': jax.random.normal(ks[1], (H, D, A), dtype=jnp.float32) * INIT_STD, 'Wk': jax.random.normal(ks[2], (H, D, A), dtype=jnp.float32) * INIT_STD, 'Wv': jax.random.normal(ks[3], (H, D, A), dtype=jnp.float32) * INIT_STD, 'Wo': jax.random.normal(ks[4], (H, A, D), dtype=jnp.float32) * INIT_STD, 'bq': jnp.zeros((H, A), dtype=jnp.float32), 'bk': jnp.zeros((H, A), dtype=jnp.float32), 'bv': jnp.zeros((H, A), dtype=jnp.float32), 'bo': jnp.zeros((D,), dtype=jnp.float32)}
    _L0_attn_b_in = _L0_attn_b_setup()

    def _L0_ffn_setup():
        import jax, jax.numpy as jnp
        import numpy as np
        DIM = 128
        HIDDEN = 384
        SCALE = 1.0 / 127.0

        def _dequant(w_int, dtype):
            return w_int.astype(dtype) * jnp.asarray(SCALE, dtype)
        key = jax.random.key(seed)
        k_x, k_g, k_u, k_d = jax.random.split(key, 4)
        x = jax.random.normal(k_x, (4, 256, DIM), dtype=jnp.float32)
        w_gate = jax.random.randint(k_g, (HIDDEN, DIM), -127, 128, dtype=jnp.int32)
        w_up = jax.random.randint(k_u, (HIDDEN, DIM), -127, 128, dtype=jnp.int32)
        w_down = jax.random.randint(k_d, (DIM, HIDDEN), -127, 128, dtype=jnp.int32)
        return {'x': x, 'w_gate': w_gate, 'w_up': w_up, 'w_down': w_down}
    _L0_ffn_in = _L0_ffn_setup()
    _d = {'L0_attn_a_x': _L0_attn_a_in['x'], 'L0_attn_a_Wq': _L0_attn_a_in['Wq'], 'L0_attn_a_gq': _L0_attn_a_in['gq'], 'L0_attn_a_bq': _L0_attn_a_in['bq'], 'L0_attn_a_mq': _L0_attn_a_in['mq'], 'L0_attn_a_vq': _L0_attn_a_in['vq'], 'L0_attn_a_Wk': _L0_attn_a_in['Wk'], 'L0_attn_a_gk': _L0_attn_a_in['gk'], 'L0_attn_a_bk': _L0_attn_a_in['bk'], 'L0_attn_a_mk': _L0_attn_a_in['mk'], 'L0_attn_a_vk': _L0_attn_a_in['vk'], 'L0_attn_a_Wv': _L0_attn_a_in['Wv'], 'L0_attn_a_gv': _L0_attn_a_in['gv'], 'L0_attn_a_bv': _L0_attn_a_in['bv'], 'L0_attn_a_mv': _L0_attn_a_in['mv'], 'L0_attn_a_vv': _L0_attn_a_in['vv'], 'L0_attn_a_Wo': _L0_attn_a_in['Wo'], 'L0_attn_a_bo': _L0_attn_a_in['bo'], 'L0_attn_b_Wq': _L0_attn_b_in['Wq'], 'L0_attn_b_Wk': _L0_attn_b_in['Wk'], 'L0_attn_b_Wv': _L0_attn_b_in['Wv'], 'L0_attn_b_Wo': _L0_attn_b_in['Wo'], 'L0_attn_b_bq': _L0_attn_b_in['bq'], 'L0_attn_b_bk': _L0_attn_b_in['bk'], 'L0_attn_b_bv': _L0_attn_b_in['bv'], 'L0_attn_b_bo': _L0_attn_b_in['bo'], 'L0_ffn_w_gate': _L0_ffn_in['w_gate'], 'L0_ffn_w_up': _L0_ffn_in['w_up'], 'L0_ffn_w_down': _L0_ffn_in['w_down']}
    _x0 = _d['L0_attn_a_x']
    _d['L0_attn_a_x'] = jax.random.normal(jax.random.fold_in(jax.random.key(seed), 1), (8, 256, 128), dtype=_x0.dtype)
    del _x0
    return _d

def reference(L0_attn_a_x, L0_attn_a_Wq, L0_attn_a_gq, L0_attn_a_bq, L0_attn_a_mq, L0_attn_a_vq, L0_attn_a_Wk, L0_attn_a_gk, L0_attn_a_bk, L0_attn_a_mk, L0_attn_a_vk, L0_attn_a_Wv, L0_attn_a_gv, L0_attn_a_bv, L0_attn_a_mv, L0_attn_a_vv, L0_attn_a_Wo, L0_attn_a_bo, L0_attn_b_Wq, L0_attn_b_Wk, L0_attn_b_Wv, L0_attn_b_Wo, L0_attn_b_bq, L0_attn_b_bk, L0_attn_b_bv, L0_attn_b_bo, L0_ffn_w_gate, L0_ffn_w_up, L0_ffn_w_down):

    def _L0_attn_a_ref(x, Wq, gq, bq, mq, vq, Wk, gk, bk, mk, vk, Wv, gv, bv, mv, vv, Wo, bo):
        import jax, jax.numpy as jnp
        import numpy as np
        B, N, D = (8, 256, 128)
        A_STDP, TAU_STDP, W_OFF, T_MAX = (0.9, 0.5, 0.9, 1.0)
        V_TH, EPS = (1.0, 1e-05)

        def _proj(x, W, g, b, m, v):
            h = x @ W
            h = (h - m) * (g * jax.lax.rsqrt(v + EPS)) + b
            return jax.nn.sigmoid(4.0 * (h - V_TH))
        Q = _proj(x, Wq, gq, bq, mq, vq)
        K = _proj(x, Wk, gk, bk, mk, vk)
        V = _proj(x, Wv, gv, bv, mv, vv)
        t_Q = T_MAX * (1.0 - Q.mean(axis=-1, keepdims=True))
        t_K = T_MAX * (1.0 - K.mean(axis=-1, keepdims=True))
        delta_t = t_Q - jnp.swapaxes(t_K, 1, 2)
        f_stdp = A_STDP * jnp.exp(-jnp.abs(delta_t) / TAU_STDP)
        A = jnp.where(delta_t < 0, f_stdp, -f_stdp) + W_OFF
        return A @ V @ Wo + bo

    def _L0_attn_b_ref(residual, Wq, Wk, Wv, Wo, bq, bk, bv, bo):
        import jax, jax.numpy as jnp
        import numpy as np
        B, S, D, H, A = (2, 256, 128, 16, 64)
        INIT_STD = 0.02
        q = jnp.einsum('bsd,hda->bhsa', residual, Wq) + bq[None, :, None, :]
        k = jnp.einsum('bsd,hda->bhsa', residual, Wk) + bk[None, :, None, :]
        v = jnp.einsum('bsd,hda->bhsa', residual, Wv) + bv[None, :, None, :]
        scale = 1.0 / jnp.sqrt(jnp.float32(q.shape[-1]))
        scores = jnp.einsum('bhsa,bhta->bhst', q, k) * scale
        s = scores.shape[-1]
        causal = jnp.tril(jnp.ones((s, s), dtype=bool))
        masked = jnp.where(causal, scores, jnp.float32(-100000.0))
        pattern = jax.nn.softmax(masked, axis=-1)
        z = jnp.einsum('bhst,bhta->bshа'.replace('а', 'a'), pattern, v)
        out = jnp.einsum('bsha,had->bsd', z, Wo) + bo
        return out

    def _L0_ffn_ref(x, w_gate, w_up, w_down):
        import jax, jax.numpy as jnp
        import numpy as np
        DIM = 128
        HIDDEN = 384
        SCALE = 1.0 / 127.0

        def _dequant(w_int, dtype):
            return w_int.astype(dtype) * jnp.asarray(SCALE, dtype)
        wg = _dequant(w_gate, x.dtype)
        wu = _dequant(w_up, x.dtype)
        wd = _dequant(w_down, x.dtype)
        gate = jnp.einsum('bsd,hd->bsh', x, wg)
        up = jnp.einsum('bsd,hd->bsh', x, wu)
        h = jax.nn.silu(gate) * up
        return jnp.einsum('bsh,dh->bsd', h, wd)
    x = L0_attn_a_x
    x = x + _L0_attn_a_ref(_layernorm(x, axis=-1), L0_attn_a_Wq, L0_attn_a_gq, L0_attn_a_bq, L0_attn_a_mq, L0_attn_a_vq, L0_attn_a_Wk, L0_attn_a_gk, L0_attn_a_bk, L0_attn_a_mk, L0_attn_a_vk, L0_attn_a_Wv, L0_attn_a_gv, L0_attn_a_bv, L0_attn_a_mv, L0_attn_a_vv, L0_attn_a_Wo, L0_attn_a_bo)
    x = x + _L0_ffn_ref(_layernorm(x, axis=-1), L0_ffn_w_gate, L0_ffn_w_up, L0_ffn_w_down)
    x = x + _L0_attn_b_ref(_layernorm(x, axis=-1), L0_attn_b_Wq, L0_attn_b_Wk, L0_attn_b_Wv, L0_attn_b_Wo, L0_attn_b_bq, L0_attn_b_bk, L0_attn_b_bv, L0_attn_b_bo)
    x = x + _L0_ffn_ref(_layernorm(x, axis=-1), L0_ffn_w_gate, L0_ffn_w_up, L0_ffn_w_down)
    return x

_drawn_inputs = setup_inputs


def setup_inputs(seed=0):
    import zlib

    import numpy as np

    out = dict(_drawn_inputs(seed))
    spreads = {'L0_attn_a_gq': (1.0, 0.2),
     'L0_attn_a_bq': (0.0, 0.1),
     'L0_attn_a_mq': (0.0, 0.1),
     'L0_attn_a_vq': (1.0, 0.2),
     'L0_attn_a_gk': (1.0, 0.2),
     'L0_attn_a_bk': (0.0, 0.1),
     'L0_attn_a_mk': (0.0, 0.1),
     'L0_attn_a_vk': (1.0, 0.2),
     'L0_attn_a_gv': (1.0, 0.2),
     'L0_attn_a_bv': (0.0, 0.1),
     'L0_attn_a_mv': (0.0, 0.1),
     'L0_attn_a_vv': (1.0, 0.2),
     'L0_attn_a_bo': (0.0, 0.1),
     'L0_attn_b_bq': (0.0, 2.0),
     'L0_attn_b_bk': (0.0, 2.0),
     'L0_attn_b_bv': (0.0, 2.0),
     'L0_attn_b_bo': (0.0, 2.0)}
    factors = {'L0_attn_b_Wq': 25.886, 'L0_attn_b_Wk': 24.699, 'L0_attn_b_Wv': 8.0, 'L0_attn_b_Wo': 8.0}
    for name, (base, spread) in spreads.items():
        noise = np.random.default_rng([zlib.crc32(name.encode()), seed]).standard_normal(out[name].shape)
        drawn = base * np.exp(spread * noise) if base else spread * noise
        out[name] = jnp.asarray(drawn.astype(out[name].dtype))
    for name, factor in factors.items():
        out[name] = (out[name] * factor).astype(out[name].dtype)
    return out
```

```python
from contextlib import ExitStack

import concourse.bass as bass
from concourse import mybir

P = 128
ALU = mybir.AluOpType
ACT = mybir.ActivationFunctionType
F32 = mybir.dt.float32
F32R = mybir.dt.float32r
I32 = mybir.dt.int32

B, N, D = 8, 256, 128
H, A = 16, 64
F = 384
PAIR = 2 * N
PAIRS = B * N // PAIR
TILES = PAIR // P
FC = F // P
STEPS = 2 * H
GH = PAIR // D
GROUPS = H // GH
CH = GROUPS * TILES
SC = N + P
EPS = 1e-5
W_SCALE = 1.0 / 127.0
SCORE_SCALE = A ** -0.5
A_STDP, W_OFF, INV_TAU = 0.9, 0.9, 2.0
BIG = 1e30

BODY = {
    1: [("bout", -1)], 2: [("lns", -1)], 4: [("lntF", -1)], 5: [("gu0", -1)], 6: [("gu1", -1)],
    7: [("gu2", -1)], 9: [("down", -1), ("lns", 1)], 11: [("lntA", 1)], 12: [("qkv0", 1)],
    13: [("qkv1", 1)], 14: [("qkv2", 1)], 15: [("mean", 1)], 16: [("vwo", 1), ("mat", 1)],
    19: [("aout", 1)], 20: [("lns", 1)], 22: [("lntF", 1)], 23: [("gu0", 1)], 24: [("gu1", 1)],
    25: [("gu2", 1)], 27: [("down", 1)], 28: [("lns", 1)], 32: [("lntB", 1)],
}
PROLOGUE = ["lns", "w0", "lntA", "w1", "qkv0", "qkv1", "qkv2", "w2", "mean", "vwo", "mat", "w3", "w4",
            "aout", "lns", "w5", "lntF", "gu0", "w6", "gu1", "w7", "gu2", "wb", "down", "lns", "lntB"]
EPILOGUE = ["bout", "lns", "lntF", "gu0", "gu1", "gu2", "down"]


USES = {"lntA": (1, 0), "lntF": (1, 0), "lntB": (1, 0), "qkv0": (0, 1), "qkv1": (1, 0), "qkv2": (0, 1), "mean": (1, 1),
        "vwo": (1, 0), "aout": (0, 1), "gu0": (1, 1), "gu1": (1, 1), "gu2": (1, 1), "down": (1, 0), "bout": (1, 0)}


WEIGHTS = [f"w{i}" for i in range(8)]


class Tally:

    def __init__(self):
        self.ln = 0
        self.xt = 0
        self.x = 0
        self.y = 0
        self.a = 0
        self.f = 0
        self.o = 0
        self.link = 0

    def passed(self, job):
        uses_x, uses_y = USES.get(job, (0, 0))
        self.x += uses_x
        self.y += uses_y
        self.ln += job == "lns"
        self.xt += job in ("lntA", "lntF")
        self.a += job == "aout"
        self.f += job == "down"
        self.o += job == "bout"


def build(nc, x_d, wa_d, ga_d, woa_d, boa_d, wq_d, wk_d, wv_d, wo_d, bq_d, bv_d, bo_d, wg_d, wu_d, wd_d, out_d):
    x_view = x_d.rearrange("(t p) d -> p t d", p=P)
    out_view = out_d.rearrange("(t p) d -> p t d", p=P)

    with ExitStack() as ctx:
        def sb(name, shape, dt=F32):
            return ctx.enter_context(nc.sbuf_tensor(name, shape, dt))

        def sem(name):
            return ctx.enter_context(nc.semaphore(name))

        wa = sb("wa", [P, 3, D])
        wa_hi, wa_lo = sb("wa_hi", [P, 3, D], F32R), sb("wa_lo", [P, 3, D], F32R)
        ga = sb("ga", [P, 4, 3])
        ga_scale, ga_bias, ga_rs, ga_tmp = sb("ga_scale", [P, 3]), sb("ga_bias", [P, 3]), sb("ga_rs", [P, 3]), sb("ga_tmp", [P, 3])
        woa, boa = sb("woa", [P, D]), sb("boa", [P, D])
        wqT, wkT, wvT, wo = (sb(n, [A, H, D]) for n in ("wqT", "wkT", "wvT", "wo"))
        bqT, bvT, bo = sb("bqT", [A, H]), sb("bvT", [A, H]), sb("bo", [P, 1])
        m_hi, m_lo = sb("m_hi", [P, H, D], F32R), sb("m_lo", [P, H, D], F32R)
        wvo_hi, wvo_lo = sb("wvo_hi", [P, H, D], F32R), sb("wvo_lo", [P, H, D], F32R)
        u_bias, o_bias = sb("u_bias", [P, H]), sb("o_bias", [P, 1])
        wg_i, wu_i, wd_i = sb("wg_i", [P, F], I32), sb("wu_i", [P, F], I32), sb("wd_i", [P, FC, D], I32)
        wg, wu, wd = sb("wg", [P, F], F32R), sb("wu", [P, F], F32R), sb("wd", [P, FC, D])
        ident = sb("ident", [P, P])
        mask = sb("mask", [P, N])
        mean_w = sb("mean_w", [P, P])
        minus_half = sb("minus_half", [P, TILES])

        x = sb("x", [P, PAIRS * TILES, D])
        stats, mv, var, rstd = sb("stats", [P, TILES, 6]), sb("mv", [P, TILES, 2]), sb("var", [P, TILES]), sb("rstd", [P, TILES])
        xn = sb("xn", [P, TILES, D])
        xt_hi, xt_lo = sb("xt_hi", [P, PAIR], F32R), sb("xt_lo", [P, PAIR], F32R)
        rt_hi, rt_lo, rt = sb("rt_hi", [P, PAIR], F32R), sb("rt_lo", [P, PAIR], F32R), sb("rt", [P, PAIR])
        t_qkv = sb("t_qkv", [P, 3, PAIR])
        sv, tq, ntk, vwo = sb("sv", [P, PAIR]), sb("tq", [P, PAIR]), sb("ntk", [P, TILES]), sb("vwo", [P, TILES, D])
        dist, expd, less, signed, stdp = (sb(n, [P, TILES, N]) for n in ("dist", "expd", "less", "signed", "stdp"))
        xb = sb("xb", [P, TILES, D])
        gate_t, gated, hid = sb("gate_t", [P, PAIR]), sb("gated", [P, PAIR]), sb("hid", [P, FC, PAIR])
        u = sb("u", [P, 2, PAIR])
        v = sb("v", [P, 2, TILES, GH * D])
        neg_s = sb("neg_s", [P, 2, SC])
        neg_max, row_sum, row_inv = sb("neg_max", [P, 4, 2]), sb("row_sum", [P, 4, 2]), sb("row_inv", [P, 4, 2])
        prob = sb("prob", [P, 4, SC])
        prob_t = sb("prob_t", [P, 2, SC])
        o_t = sb("o_t", [P, PAIR])

        bank = [ctx.enter_context(nc.psum_tensor(f"bank{i}", [P, 512], F32)) for i in range(8)]
        s_ps, pt_ps, u_ps, v_ps, o_ps, X, Y = bank[0:2], bank[2], bank[3], bank[4], bank[5], bank[6], bank[7]

        ld_x, ld_a, ld_f, ld_b = sem("ld_x"), sem("ld_a"), sem("ld_f"), sem("ld_b")
        consts = sem("consts")
        consts_in = sem("consts_in")
        wa_ready, ga_v, ga_pow, ga_ready, wf_ready = sem("wa_ready"), sem("ga_v"), sem("ga_pow"), sem("ga_ready"), sem("wf_ready")
        w_full, w_hi, w_lo = sem("w_full"), sem("w_hi"), sem("w_lo")
        link_s = sem("link")
        ln_var, ln_rstd, xn_ready = sem("ln_var"), sem("ln_rstd"), sem("xn_ready")
        xt_hi_s = sem("xt_hi_s")
        x_full, x_free, y_full, y_free = sem("x_full"), sem("x_free"), sem("y_full"), sem("y_free")
        sv_s, dist_s, exp_s, sign_s, stdp_s, xb_s = (sem(n) for n in ("sv_s", "dist_s", "exp_s", "sign_s", "stdp_s", "xb_s"))
        gate_s, rt_hi_s = sem("gate_s"), sem("rt_hi_s")
        u_full, u_sb, v_full, v_sb = sem("u_full"), sem("u_sb"), sem("v_full"), sem("v_sb")
        s_full, s_masked, p_exp, p_inv, p_norm = sem("s_full"), sem("s_masked"), sem("p_exp"), sem("p_inv"), sem("p_norm")
        pt_full, pt_sb, pv_done, o_sb = sem("pt_full"), sem("pt_sb"), sem("pv_done"), sem("o_sb")
        stored = sem("stored")

        def chunk_of(step):
            g, r = divmod(step, 2 * GH)
            return (g + 1) * TILES + r // 2 if r % 2 and g + 1 < GROUPS else None

        def pairs(side, main):
            at = Tally()
            for job in PROLOGUE:
                side(job, 0, at)
                at.passed(job)
            for p in range(PAIRS):
                for step in range(-1, STEPS + 3):
                    main(p, step, at)
                    for job, off in BODY.get(step, []):
                        if 0 <= p + off < PAIRS:
                            side(job, p + off, at)
                            at.passed(job)
            for job in EPILOGUE:
                side(job, PAIRS - 1, at)
                at.passed(job)

        block = ctx.enter_context(nc.Block())

        @block.sync
        def _(sp):
            sp.dma_start(x[:, 0:TILES, :], x_view[:, 0:TILES, :]).then_inc(ld_x, 16)
            sp.dma_start(ga[:], ga_d).then_inc(ld_a, 16)
            sp.dma_start(wa[:], wa_d).then_inc(ld_a, 16)
            sp.dma_start(woa[:], woa_d).then_inc(ld_a, 16)
            sp.dma_start(boa[:], boa_d).then_inc(ld_a, 16)
            for dst, src in ((wvT, wv_d), (wo, wo_d)):
                sp.dma_start(dst[:], src).then_inc(ld_b, 16)
            for dst, src in ((wg_i, wg_d), (wu_i, wu_d), (wd_i, wd_d)):
                sp.dma_start(dst[:], src).then_inc(ld_f, 16)
            for p in range(1, PAIRS):
                sp.dma_start(x[:, p * TILES:(p + 1) * TILES, :], x_view[:, p * TILES:(p + 1) * TILES, :]).then_inc(ld_x, 16)

            def side(job, p, at):
                if job == "down" and at.o == p + 1:
                    sp.wait_ge(x_free, at.x + 1)
                    ts = bass.ds(p * TILES, TILES)
                    sp.dma_start(out_view[:, ts, :], x[:, ts, :]).then_inc(stored, 16)

            pairs(side, lambda p, step, at: None)
            sp.wait_ge(stored, 16 * PAIRS)

        @block.tensor
        def _(pe):
            def split3(out, w_hi_ap, w_lo_ap, r_hi_ap, r_lo_ap):
                nc.tensor.matmul(out, w_hi_ap, r_hi_ap, start=True, stop=False)
                nc.tensor.matmul(out, w_lo_ap, r_hi_ap, start=False, stop=False)
                return nc.tensor.matmul(out, w_hi_ap, r_lo_ap, start=False, stop=True)

            def use_x(at):
                if isinstance(at.x, int) and at.x == 0:
                    return
                pe.wait_ge(x_free, at.x)

            def use_y(at):
                if isinstance(at.y, int) and at.y == 0:
                    return
                pe.wait_ge(y_free, at.y)

            def side(job, p, at):
                if job == "lns":
                    pass
                elif job in ("lntA", "lntF", "lntB"):
                    if at.ln == 1:
                        pe.wait_ge(consts, 1)
                    pe.wait_ge(xn_ready, at.ln)
                    use_x(at)
                    for j in range(TILES):
                        last = nc.tensor.transpose(X[:, j * P:(j + 1) * P], xn[:, j, :], ident[:])
                    last.then_inc(x_full, 1)
                    if job != "lntB":
                        pass
                elif job.startswith("qkv"):
                    w = int(job[3])
                    if w == 0:
                        pe.wait_ge(wa_ready, 1)
                        pe.wait_ge(x_free, at.x)
                    if w == 1:
                        use_x(at)
                        split3(X[:], wa_hi[:, w, :], wa_lo[:, w, :], xt_hi[:], xt_lo[:]).then_inc(x_full, 1)
                    else:
                        use_y(at)
                        split3(Y[:], wa_hi[:, w, :], wa_lo[:, w, :], xt_hi[:], xt_lo[:]).then_inc(y_full, 1)
                elif job == "mean":
                    use_x(at)
                    use_y(at)
                    nc.tensor.matmul(X[:], mean_w[:], t_qkv[:, 0, :], start=True, stop=True).then_inc(x_full, 1)
                    for j in range(TILES):
                        last = nc.tensor.matmul(Y[:, j:j + 1], t_qkv[:, 1, j * P:(j + 1) * P], mean_w[:, 0:1], start=True, stop=True)
                    last.then_inc(y_full, 1)
                elif job == "vwo":
                    pe.wait_ge(sv_s, at.a + 1)
                    use_x(at)
                    for j in range(TILES):
                        last = nc.tensor.matmul(X[:, j * D:(j + 1) * D], sv[:, j * P:(j + 1) * P], woa[:], start=True, stop=True)
                    last.then_inc(x_full, 1)
                elif job == "aout":
                    pe.wait_ge(x_free, at.x)
                    pe.wait_ge(stdp_s, at.a + 1)
                    use_y(at)
                    for q in range(TILES):
                        b, qt = divmod(q, 2)
                        for kt in range(2):
                            last = nc.tensor.matmul(Y[:, q * D:(q + 1) * D], stdp[:, 2 * b + kt, qt * P:(qt + 1) * P],
                                                    vwo[:, 2 * b + kt, :], start=(kt == 0), stop=(kt == 1))
                    last.then_inc(y_full, 1)
                elif job.startswith("gu"):
                    c = int(job[2])
                    if c == 0:
                        pe.wait_ge(wf_ready, 1)
                        pe.wait_ge(x_free, at.x)
                    cs = slice(c * P, (c + 1) * P)
                    use_x(at)
                    nc.tensor.matmul(X[:], wg[:, cs], xt_hi[:], start=True, stop=False)
                    nc.tensor.matmul(X[:], wg[:, cs], xt_lo[:], start=False, stop=True).then_inc(x_full, 1)
                    use_y(at)
                    nc.tensor.matmul(Y[:], wu[:, cs], xt_hi[:], start=True, stop=False)
                    nc.tensor.matmul(Y[:], wu[:, cs], xt_lo[:], start=False, stop=True).then_inc(y_full, 1)
                elif job == "down":
                    pe.wait_ge(y_free, at.y)
                    use_x(at)
                    for j in range(TILES):
                        for c in range(FC):
                            last = nc.tensor.matmul(X[:, j * D:(j + 1) * D], hid[:, c, j * P:(j + 1) * P], wd[:, c, :],
                                                    start=(c == 0), stop=(c == FC - 1))
                    last.then_inc(x_full, 1)
                elif job == "bout":
                    pe.wait_ge(o_sb, at.o + 1)
                    use_x(at)
                    for j in range(TILES):
                        last = nc.tensor.transpose(X[:, j * P:(j + 1) * P], o_t[:, j * P:(j + 1) * P], ident[:])
                    last.then_inc(x_full, 1)
                elif job == "wb":
                    pe.wait_ge(w_lo, 8)
                    for h in range(H):
                        nc.tensor.matmul(v_ps[:, h:h + 1], wkT[:, h, :], bqT[:, h:h + 1], start=True, stop=True)
                    for h in range(H):
                        last = nc.tensor.matmul(v_ps[:, H:H + 1], wo[:, h, :], bvT[:, h:h + 1], start=(h == 0), stop=(h == H - 1))
                    last.then_inc(w_full, 1)
                elif job in WEIGHTS:
                    i = int(job[1])
                    if i == 0:
                        pe.wait_ge(ld_b, 16 * 7)
                    if i >= 2:
                        pe.wait_ge(w_lo, i - 1)
                    left, right = (wvT, wo) if i < 4 else (wqT, wkT)
                    for j in range(4):
                        h = 4 * (i % 4) + j
                        last = nc.tensor.matmul((u_ps, v_ps)[i % 2][:, j * D:(j + 1) * D], left[:, h, :], right[:, h, :], start=True, stop=True)
                    last.then_inc(w_full, 1)

            def u_proj(p, h, at):
                if h == 0:
                    pe.wait_ge(rt_hi_s, p + 1)
                    pe.wait_ge(x_free, at.x)
                if not (isinstance(p, int) and p == 0 and h == 0):
                    pe.wait_ge(u_sb, H * p + h)
                split3(u_ps[:], m_hi[:, h, :], m_lo[:, h, :], rt_hi[:], rt_lo[:]).then_inc(u_full, 1)

            def v_proj(p, c):
                g, j = divmod(c, TILES)
                if not (isinstance(p, int) and p == 0 and c == 0):
                    pe.wait_ge(v_sb, CH * p + c)
                hs = slice(GH * g, GH * (g + 1))
                js = slice(j * P, (j + 1) * P)
                split3(v_ps[:], rt_hi[:, js], rt_lo[:, js], wvo_hi[:, hs, :], wvo_lo[:, hs, :]).then_inc(v_full, 1)

            def split3v(out, a_hi, a_lo, b_hi, b_lo):
                return split3(out, a_hi, a_lo, b_hi, b_lo)

            def main(p, step, at):
                if step == -1:
                    if p == 0:
                        pe.wait_ge(w_hi, 9)
                        pe.wait_ge(w_lo, 8)
                    u_proj(p, 0, at)
                    v_proj(p, 0)
                    v_proj(p, 1)
                    v_proj(p, 2)
                    v_proj(p, 3)
                    return
                if step < STEPS:
                    h, b = divmod(step, 2)
                    n = STEPS * p + step
                    pe.wait_ge(u_sb, H * p + h + 1)
                    if not (isinstance(p, int) and n < 2):
                        pe.wait_ge(s_masked, n - 1)
                    S, t = s_ps[step % 2], b * N
                    nc.tensor.matmul(S[:, 0:P], u[:, h % 2, t:t + P], rt[:, t:t + P], start=True, stop=True)
                    nc.tensor.matmul(S[:, P:SC], u[:, h % 2, t + P:t + N], rt[:, t:t + N], start=True, stop=True).then_inc(s_full, 1)
                if step >= 3:
                    k = step - 3
                    h, b = divmod(k, 2)
                    n = STEPS * p + k
                    pe.wait_ge(pt_sb, n + 1)
                    pe.wait_ge(v_sb, CH * p + TILES * (h // GH) + TILES)
                    if k == 0 and not (isinstance(p, int) and p == 0):
                        pe.wait_ge(o_sb, p)
                    hs = slice((h % GH) * D, (h % GH + 1) * D)
                    vg = v[:, (h // GH) % 2]
                    nc.tensor.matmul(o_ps[:, b * N:(b + 1) * N], vg[:, 2 * b, hs], prob_t[:, k % 2, 0:N],
                                     start=(k == 0), stop=False, skip_group_check=True)
                    nc.tensor.matmul(o_ps[:, b * N + P:(b + 1) * N], vg[:, 2 * b + 1, hs], prob_t[:, k % 2, N:SC],
                                     start=False, stop=(k >= STEPS - 2), skip_group_check=True).then_inc(pv_done, 1)
                if 2 <= step < STEPS + 2:
                    k = step - 2
                    n = STEPS * p + k
                    pe.wait_ge(p_norm, n + 1)
                    if not (isinstance(p, int) and n == 0):
                        pe.wait_ge(pt_sb, n)
                    for j in range(3):
                        last = nc.tensor.transpose(pt_ps[:, j * P:(j + 1) * P], prob[:, k % 4, j * P:(j + 1) * P], ident[:])
                    last.then_inc(pt_full, 1)
                if step < STEPS and step % 2 == 0 and step // 2 + 1 < H:
                    u_proj(p, step // 2 + 1, at)
                if step < STEPS and chunk_of(step) is not None:
                    v_proj(p, chunk_of(step))

            pairs(side, main)

        @block.scalar
        def _(act):
            for dst, src in ((wqT, wq_d), (wkT, wk_d), (bqT, bq_d), (bvT, bv_d), (bo, bo_d)):
                act.dma_start(dst[:], src).then_inc(ld_b, 16)

            def side(job, p, at):
                if job == "lns":
                    pass
                elif job in ("lntA", "lntF"):
                    act.wait_ge(x_full, at.x + 1)
                    if at.xt:
                        act.wait_ge(y_full, at.y)
                    nc.scalar.activation(xt_hi[:], X[:], ACT.Copy).then_inc(xt_hi_s, 1)
                elif job == "lntB":
                    act.wait_ge(x_full, at.x + 1)
                    if not (isinstance(p, int) and p == 0):
                        act.wait_ge(u_full, H * p)
                        act.wait_ge(v_full, CH * p)
                        act.wait_ge(s_full, STEPS * p)
                    nc.scalar.activation(rt[:], X[:], ACT.Copy)
                    nc.scalar.activation(rt_hi[:], X[:], ACT.Copy).then_inc(rt_hi_s, 1)
                elif job.startswith("qkv"):
                    w = int(job[3])
                    if at.a == 0 and w == 0:
                        act.wait_ge(ga_ready, 1)
                    if w == 1:
                        act.wait_ge(x_full, at.x + 1)
                        nc.scalar.activation(t_qkv[:, w, :], X[:], ACT.Tanh, bias=ga_bias[:, w:w + 1],
                                             scale=ga_scale[:, w:w + 1]).then_inc(x_free, 1)
                    else:
                        act.wait_ge(y_full, at.y + 1)
                        if w == 2 and at.a:
                            act.wait_ge(sv_s, at.a)
                        nc.scalar.activation(t_qkv[:, w, :], Y[:], ACT.Tanh, bias=ga_bias[:, w:w + 1],
                                             scale=ga_scale[:, w:w + 1]).then_inc(y_free, 1)
                elif job == "mean":
                    pass
                elif job == "vwo":
                    act.wait_ge(x_full, at.x + 1)
                    nc.scalar.activation(vwo[:], X[:].rearrange("p (j d) -> p j d", d=D), ACT.Copy).then_inc(x_free, 1)
                elif job == "mat":
                    act.wait_ge(x_free, at.x - 1)
                    act.wait_ge(y_free, at.y)
                    for j in range(TILES):
                        b = j // 2
                        last = nc.scalar.activation(dist[:, j, :], tq[:, b * N:(b + 1) * N], ACT.Abs, bias=ntk[:, j:j + 1])
                    last.then_inc(dist_s, 1)
                    act.wait_ge(dist_s, at.a + 1)
                    nc.scalar.activation(expd[:], dist[:], ACT.Exp, scale=-INV_TAU).then_inc(exp_s, 1)
                elif job == "aout":
                    pass
                elif job.startswith("gu"):
                    c = int(job[2])
                    act.wait_ge(x_full, at.x + 1)
                    act.wait_ge(x_free, at.x)
                    nc.scalar.activation(gate_t[:], X[:], ACT.Tanh, scale=0.5 * W_SCALE).then_inc(gate_s, 1)
                elif job == "down":
                    pass
                elif job == "bout":
                    pass
                elif job == "wb":
                    act.wait_ge(w_full, 9)
                    nc.scalar.activation(u_bias[:], v_ps[:, 0:H], ACT.Copy, scale=SCORE_SCALE)
                    nc.scalar.activation(o_bias[:], v_ps[:, H:H + 1], ACT.Identity, bias=bo[:]).then_inc(w_hi, 1)
                elif job in WEIGHTS:
                    i = int(job[1])
                    act.wait_ge(w_full, i + 1)
                    dst = (wvo_hi, m_hi)[i // 4][:, 4 * (i % 4):4 * (i % 4) + 4, :]
                    nc.scalar.activation(dst, (u_ps, v_ps)[i % 2][:].rearrange("p (j d) -> p j d", d=D), ACT.Copy,
                                         scale=(1.0, SCORE_SCALE)[i // 4]).then_inc(w_hi, 1)

            def u_evac(p, h):
                act.wait_ge(u_full, H * p + h + 1)
                if not (isinstance(p, int) and p == 0 and h < 2):
                    act.wait_ge(s_full, STEPS * p + 2 * h - 2)
                nc.scalar.activation(u[:, h % 2, :], u_ps[:], ACT.Identity, bias=u_bias[:, h:h + 1]).then_inc(u_sb, 1)

            def v_evac(p, c):
                g, j = divmod(c, TILES)
                act.wait_ge(v_full, CH * p + c + 1)
                if not (isinstance(p, int) and p == 0 and g < 2):
                    act.wait_ge(pv_done, STEPS * p + 2 * GH * (g - 1))
                nc.scalar.activation(v[:, g % 2, j, :], v_ps[:], ACT.Copy).then_inc(v_sb, 1)

            def exp(p, k):
                n = STEPS * p + k
                act.wait_ge(s_masked, n + 1)
                if not (isinstance(p, int) and n < 4):
                    act.wait_ge(pt_full, n - 3)
                    act.wait_ge(p_inv, n - 3)
                q, r = k % 4, k % 2
                nc.scalar.activation(prob[:, q, 0:P], neg_s[:, r, 0:P], ACT.Exp, bias=neg_max[:, q, 0:1], scale=-1.0,
                                     accum_out=row_sum[:, q, 0:1])
                nc.scalar.activation(prob[:, q, P:SC], neg_s[:, r, P:SC], ACT.Exp, bias=neg_max[:, q, 1:2], scale=-1.0,
                                     accum_out=row_sum[:, q, 1:2]).then_inc(p_exp, 1)

            def main(p, step, at):
                if step == -1:
                    u_evac(p, 0)
                    for c in range(TILES):
                        v_evac(p, c)
                    return
                if step < STEPS:
                    if step % 2 == 0 and step // 2 + 1 < H:
                        u_evac(p, step // 2 + 1)
                    exp(p, step)
                    if chunk_of(step) is not None:
                        v_evac(p, chunk_of(step))
                if step == STEPS + 2:
                    act.wait_ge(pv_done, STEPS * (p + 1))
                    act.wait_ge(x_full, at.x)
                    nc.scalar.activation(o_t[:], o_ps[:], ACT.Identity, bias=o_bias[:]).then_inc(o_sb, 1)

            pairs(side, main)

        @block.vector
        def _(dve):
            def link(ins, at):
                ins.then_inc(link_s, 1)
                at.link += 1
                dve.wait_ge(link_s, at.link)

            def side(job, p, at):
                if job == "lns":
                    if at.ln == 0:
                        dve.wait_ge(ld_a, 64)
                        link(nc.vector.tensor_copy(wa_hi[:], wa[:]), at)
                        nc.vector.tensor_tensor(wa_lo[:], wa[:], wa_hi[:].bitcast(F32), ALU.subtract).then_inc(wa_ready, 1)
                        nc.vector.tensor_scalar(ga_tmp[:], ga[:, 3, :], EPS, None, ALU.add).then_inc(ga_v, 1)
                        dve.wait_ge(ga_pow, 1)
                        link(nc.vector.scalar_tensor_tensor(ga_scale[:], ga_rs[:], 2.0, ga[:, 0, :], ALU.mult, ALU.mult), at)
                        link(nc.vector.tensor_tensor(ga_tmp[:], ga[:, 2, :], ga_scale[:], ALU.mult), at)
                        link(nc.vector.scalar_tensor_tensor(ga_bias[:], ga[:, 1, :], 2.0, ga_tmp[:], ALU.mult, ALU.subtract), at)
                        nc.vector.tensor_scalar(ga_bias[:], ga_bias[:], -2.0, None, ALU.add).then_inc(ga_ready, 1)
                        dve.wait_ge(ld_x, 16 * PAIRS)
                    if at.ln:
                        dve.wait_ge(x_free, at.x)
                        dve.wait_ge(y_free, at.y)
                    for j in range(TILES):
                        last = nc.vector.bn_stats(stats[:, j, :], x[:, bass.ds(p * TILES + j, 1), :].rearrange("p o d -> p (o d)"))
                    link(last, at)
                    for j in range(TILES):
                        last = nc.vector.bn_aggr(mv[:, j, :], stats[:, j, :])
                    link(last, at)
                    nc.vector.tensor_scalar(var[:], mv[:, :, 1], EPS, None, ALU.add).then_inc(ln_var, 1)
                    dve.wait_ge(ln_rstd, at.ln + 1)
                    if at.ln:
                        dve.wait_ge(x_full, at.x)
                    for j in range(TILES):
                        last = nc.vector.tensor_scalar(xn[:, j, :], x[:, bass.ds(p * TILES + j, 1), :].rearrange("p o d -> p (o d)"),
                                                       mv[:, j, 0:1], rstd[:, j:j + 1], ALU.subtract, ALU.mult)
                    last.then_inc(xn_ready, 1)
                elif job in ("lntA", "lntF"):
                    dve.wait_ge(xt_hi_s, at.xt + 1)
                    nc.vector.tensor_tensor(xt_lo[:], X[:], xt_hi[:].bitcast(F32), ALU.subtract).then_inc(x_free, 1)
                elif job == "lntB":
                    dve.wait_ge(rt_hi_s, p + 1)
                    nc.vector.tensor_tensor(rt_lo[:], X[:], rt_hi[:].bitcast(F32), ALU.subtract).then_inc(x_free, 1)
                elif job.startswith("qkv"):
                    if at.a == 0 and job == "qkv2":
                        dve.wait_ge(ld_f, 48)
                        nc.vector.tensor_copy(wg[:], wg_i[:])
                        nc.vector.tensor_copy(wu[:], wu_i[:])
                        nc.vector.tensor_copy(wd[:], wd_i[:]).then_inc(wf_ready, 1)
                elif job == "mean":
                    dve.wait_ge(x_full, at.x + 1)
                    nc.vector.tensor_scalar(tq[:], X[:], 0.5, None, ALU.add).then_inc(x_free, 1)
                    dve.wait_ge(y_full, at.y + 1)
                    nc.vector.tensor_scalar(ntk[:], Y[:, 0:TILES], 0.5, -1.0, ALU.add, ALU.mult).then_inc(y_free, 1)
                elif job == "vwo":
                    pass
                elif job == "mat":
                    dve.wait_ge(x_free, at.x - 1)
                    dve.wait_ge(y_free, at.y)
                    for j in range(TILES):
                        b = j // 2
                        last = nc.vector.tensor_scalar(less[:, j, :], tq[:, b * N:(b + 1) * N], ntk[:, j:j + 1], 0.0, ALU.add, ALU.is_lt)
                    link(last, at)
                    dve.wait_ge(exp_s, at.a + 1)
                    nc.vector.scalar_tensor_tensor(signed[:], less[:], -0.5, expd[:], ALU.add, ALU.mult).then_inc(sign_s, 1)
                elif job == "aout":
                    dve.wait_ge(y_full, at.y + 1)
                    dve.wait_ge(xb_s, at.a + 1)
                    nc.vector.tensor_tensor(x[:, bass.ds(p * TILES, TILES), :], Y[:].rearrange("p (j d) -> p j d", d=D), xb[:], ALU.add).then_inc(y_free, 1)
                elif job.startswith("gu"):
                    c = int(job[2])
                    dve.wait_ge(gate_s, FC * at.f + c + 1)
                    if at.y:
                        dve.wait_ge(y_free, at.y)
                    nc.vector.scalar_tensor_tensor(gated[:], gate_t[:], 1.0, X[:], ALU.add, ALU.mult).then_inc(x_free, 1)
                    dve.wait_ge(x_free, at.x + 1)
                    dve.wait_ge(y_full, at.y + 1)
                    nc.vector.tensor_tensor(hid[:, c, :], gated[:], Y[:], ALU.mult).then_inc(y_free, 1)
                elif job == "down":
                    dve.wait_ge(x_full, at.x + 1)
                    xs = x[:, bass.ds(p * TILES, TILES), :]
                    nc.vector.scalar_tensor_tensor(xs, X[:].rearrange("p (j d) -> p j d", d=D), 0.5 * W_SCALE ** 3, xs,
                                                   ALU.mult, ALU.add).then_inc(x_free, 1)
                elif job == "bout":
                    dve.wait_ge(x_full, at.x + 1)
                    xs = x[:, bass.ds(p * TILES, TILES), :]
                    nc.vector.tensor_tensor(xs, X[:].rearrange("p (j d) -> p j d", d=D), xs, ALU.add).then_inc(x_free, 1)
                elif job == "wb":
                    pass
                elif job in WEIGHTS:
                    i = int(job[1])
                    dve.wait_ge(w_hi, i + 1)
                    hs = slice(4 * (i % 4), 4 * (i % 4) + 4)
                    hi, lo = ((wvo_hi, wvo_lo), (m_hi, m_lo))[i // 4]
                    nc.vector.scalar_tensor_tensor(lo[:, hs, :], (u_ps, v_ps)[i % 2][:].rearrange("p (j d) -> p j d", d=D),
                                                   (1.0, SCORE_SCALE)[i // 4], hi[:, hs, :].bitcast(F32), ALU.mult, ALU.subtract).then_inc(w_lo, 1)

            def main(p, step, at):
                if step == 0 and isinstance(p, int) and p == 0:
                    dve.wait_ge(consts, 2)
                if 0 <= step < STEPS:
                    n = STEPS * p + step
                    dve.wait_ge(s_full, n + 1)
                    if not (isinstance(p, int) and n < 2):
                        dve.wait_ge(p_exp, n - 1)
                    r, q = step % 2, step % 4
                    nc.vector.tensor_tensor_reduce(out=neg_s[:, r, 0:P], in0=s_ps[r][:, 0:P], in1=mask[:, P:N], scale=-1.0, scalar=3e38,
                                                   op0=ALU.add, op1=ALU.min, accum_out=neg_max[:, q, 0:1])
                    nc.vector.tensor_tensor_reduce(out=neg_s[:, r, P:SC], in0=s_ps[r][:, P:SC], in1=mask[:], scale=-1.0, scalar=3e38,
                                                   op0=ALU.add, op1=ALU.min, accum_out=neg_max[:, q, 1:2]).then_inc(s_masked, 1)
                if 2 <= step < STEPS + 2:
                    k = step - 2
                    n = STEPS * p + k
                    dve.wait_ge(pt_full, n + 1)
                    if not (isinstance(p, int) and n < 2):
                        dve.wait_ge(pv_done, n - 1)
                    nc.vector.tensor_copy(prob_t[:, k % 2, :], pt_ps[:, 0:SC]).then_inc(pt_sb, 1)
                if 1 <= step < STEPS + 1:
                    k = step - 1
                    dve.wait_ge(p_exp, STEPS * p + k + 1)
                    nc.vector.reciprocal(row_inv[:, k % 4, :], row_sum[:, k % 4, :]).then_inc(p_inv, 1)

            pairs(side, main)

        @block.gpsimd
        def _(pool):
            nc.gpsimd.memset(ident[:], 0.0).then_inc(consts_in, 1)
            nc.gpsimd.memset(mask[:], 0.0).then_inc(consts_in, 1)
            nc.gpsimd.memset(mean_w[:], -0.5 / D).then_inc(consts_in, 1)
            nc.gpsimd.memset(minus_half[:], -0.5).then_inc(consts_in, 1)
            pool.wait_ge(consts_in, 4)
            nc.gpsimd.affine_select(out=ident[:], in_=ident[:], compare_op=ALU.not_equal, fill=1.0, base=0,
                                    pattern=[[-1, P]], channel_multiplier=1).then_inc(consts, 1)
            nc.gpsimd.affine_select(out=mask[:, P:N], in_=mask[:, P:N], compare_op=ALU.is_ge, fill=-BIG, base=0,
                                    pattern=[[-1, P]], channel_multiplier=1).then_inc(consts, 1)
            pool.wait_ge(ga_v, 1)
            for w in range(1):
                nc.gpsimd.tensor_tensor(ga_rs[:], ga_tmp[:], minus_half[:, 0:3], ALU.pow).then_inc(ga_pow, 1)

            def side(job, p, at):
                if job == "lns":
                    pool.wait_ge(ln_var, at.ln + 1)
                    nc.gpsimd.tensor_tensor(rstd[:], var[:], minus_half[:], ALU.pow).then_inc(ln_rstd, 1)
                elif job == "qkv2":
                    pool.wait_ge(y_free, at.y + 1)
                    nc.gpsimd.tensor_scalar(sv[:], t_qkv[:, 2, :], 0.5, 0.5, ALU.mult, ALU.add).then_inc(sv_s, 1)
                elif job == "mat":
                    nc.gpsimd.tensor_tensor(xb[:], x[:, bass.ds(p * TILES, TILES), :], boa[:, :].unsqueeze(1).to_broadcast([P, TILES, D]), ALU.add).then_inc(xb_s, 1)
                    pool.wait_ge(sign_s, at.a + 1)
                    nc.gpsimd.tensor_scalar(stdp[:], signed[:], 2.0 * A_STDP, W_OFF, ALU.mult, ALU.add).then_inc(stdp_s, 1)
                elif job == "aout":
                    pass

            def main(p, step, at):
                if 1 <= step < STEPS + 1:
                    k = step - 1
                    pool.wait_ge(p_inv, STEPS * p + k + 1)
                    q = k % 4
                    nc.gpsimd.tensor_scalar(prob[:, q, 0:P], prob[:, q, 0:P], row_inv[:, q, 0:1], None, ALU.mult)
                    nc.gpsimd.tensor_scalar(prob[:, q, P:SC], prob[:, q, P:SC], row_inv[:, q, 1:2], None, ALU.mult).then_inc(p_norm, 1)

            pairs(side, main)


def kernel(**inputs):
    import numpy as np
    import concourse.bacc as bacc
    from concourse.bass_utils import run_bass_kernel_spmd

    a = {k.removeprefix("L0_"): np.asarray(v) for k, v in inputs.items()}
    x = a["attn_a_x"]
    arrays = {
        "x": x.reshape(B * N, D),
        "wa": np.stack([a[f"attn_a_W{c}"] for c in "qkv"], 1),
        "ga": np.stack([np.stack([a[f"attn_a_{n}{c}"] for c in "qkv"], 1) for n in "gbmv"], 1),
        "woa": a["attn_a_Wo"],
        "boa": np.tile(a["attn_a_bo"][None, :], (P, 1)),
        "wq": a["attn_b_Wq"].transpose(2, 0, 1),
        "wk": a["attn_b_Wk"].transpose(2, 0, 1),
        "wv": a["attn_b_Wv"].transpose(2, 0, 1),
        "wo": a["attn_b_Wo"].transpose(1, 0, 2),
        "bq": a["attn_b_bq"].T,
        "bv": a["attn_b_bv"].T,
        "bo": a["attn_b_bo"][:, None],
        "wg": a["ffn_w_gate"].T,
        "wu": a["ffn_w_up"].T,
        "wd": a["ffn_w_down"].T.reshape(FC, P, D).transpose(1, 0, 2),
    }
    arrays = {f"{k}_in": np.ascontiguousarray(v) for k, v in arrays.items()}
    nc = bacc.Bacc("TRN2", target_bir_lowering=False, num_devices=1)
    args = [nc.dram_tensor(k, v.shape, mybir.dt.from_np(v.dtype), kind="ExternalInput").ap() for k, v in arrays.items()]
    out = nc.dram_tensor("out", (B * N, D), F32, kind="ExternalOutput").ap()
    build(nc, *args, out)
    r = run_bass_kernel_spmd(nc, [arrays], core_ids=[0])
    return r.results[0]["out"].reshape(x.shape)
```

```python
from contextlib import ExitStack

import concourse.bass as bass
from concourse import mybir

P = 128
ALU = mybir.AluOpType
ACT = mybir.ActivationFunctionType
F32 = mybir.dt.float32
F32R = mybir.dt.float32r
I32 = mybir.dt.int32

B, N, D = 8, 256, 128
H, A = 16, 64
F = 384
PAIR = 2 * N
PAIRS = B * N // PAIR
TILES = PAIR // P
FC = F // P
STEPS = 2 * H
GH = PAIR // D
GROUPS = H // GH
CH = GROUPS * TILES
SC = N + P
EPS = 1e-5
W_SCALE = 1.0 / 127.0
SCORE_SCALE = A ** -0.5
A_STDP, W_OFF, INV_TAU = 0.9, 0.9, 2.0
BIG = 1e30

BODY = {
    1: [("bout", -1)], 2: [("lns0", -1)], 3: [("lns1", -1)], 4: [("lntF", -1)], 5: [("gu0", -1)], 6: [("gu1", -1)],
    7: [("gu2", -1)], 9: [("down", -1), ("lns0", 1)], 10: [("lns1", 1)], 11: [("lntA", 1)], 12: [("qkv0", 1)],
    13: [("qkv1", 1)], 14: [("qkv2", 1)], 15: [("mean", 1)], 16: [("vwo", 1), ("mat0", 1)], 18: [("mat1", 1)],
    19: [("aout", 1)], 20: [("lns0", 1)], 21: [("lns1", 1)], 22: [("lntF", 1)], 23: [("gu0", 1)], 24: [("gu1", 1)],
    25: [("gu2", 1)], 27: [("down", 1)], 28: [("lns0", 1)], 29: [("lns1", 1)], 32: [("lntB", 1)],
}
A_STEPS = range(9, 20)
PROLOGUE = [("lns0", 0), ("lns1", 0), ("w0", 0), ("w1", 0), ("lntA", 0), ("qkv0", 0), ("qkv1", 0), ("qkv2", 0), ("w2", 0),
            ("mean", 0), ("vwo", 0), ("mat0", 0), ("lns0", 1), ("lns1", 1), ("w3", 0), ("w4", 0), ("mat1", 0), ("lntA", 1),
            ("w5", 0), ("aout", 0), ("qkv0", 1), ("lns0", 0), ("lns1", 0), ("qkv1", 1), ("qkv2", 1), ("w6", 0), ("lntF", 0),
            ("mean", 1), ("vwo", 1), ("gu0", 0), ("w7", 0), ("gu1", 0), ("wb", 0), ("mat0", 1), ("gu2", 0), ("mat1", 1),
            ("down", 0), ("lns0", 0), ("lns1", 0), ("aout", 1), ("lntB", 0)]
EPILOGUE = ["bout", "lns0", "lns1", "lntF", "gu0", "gu1", "gu2", "down"]

USES = {"lntA": (1, 0), "lntF": (1, 0), "lntB": (1, 0), "qkv0": (0, 1), "qkv1": (1, 0), "qkv2": (0, 1), "mean": (1, 1),
        "vwo": (1, 0), "aout": (0, 1), "gu0": (1, 1), "gu1": (1, 1), "gu2": (1, 1), "down": (1, 0), "bout": (1, 0)}


WEIGHTS = [f"w{i}" for i in range(8)]


class Tally:

    def __init__(self):
        self.ln = 0
        self.xt = 0
        self.x = 0
        self.y = 0
        self.a = 0
        self.f = 0
        self.o = 0
        self.link = 0

    def passed(self, job):
        uses_x, uses_y = USES.get(job, (0, 0))
        self.x += uses_x
        self.y += uses_y
        self.ln += job == "lns1"
        self.xt += job in ("lntA", "lntF")
        self.a += job == "aout"
        self.f += job == "down"
        self.o += job == "bout"


def build(nc, x_d, wa_d, ga_d, woa_d, boa_d, wq_d, wk_d, wv_d, wo_d, bq_d, bv_d, bo_d, wg_d, wu_d, wd_d, out_d):
    x_view = x_d.rearrange("(t p) d -> p t d", p=P)
    out_view = out_d.rearrange("(t p) d -> p t d", p=P)

    with ExitStack() as ctx:
        def sb(name, shape, dt=F32):
            return ctx.enter_context(nc.sbuf_tensor(name, shape, dt))

        def sem(name):
            return ctx.enter_context(nc.semaphore(name))

        wa = sb("wa", [P, 3, D])
        wa_hi, wa_lo = sb("wa_hi", [P, 3, D], F32R), sb("wa_lo", [P, 3, D], F32R)
        ga = sb("ga", [P, 4, 3])
        ga_scale, ga_bias, ga_rs, ga_tmp = sb("ga_scale", [P, 3]), sb("ga_bias", [P, 3]), sb("ga_rs", [P, 3]), sb("ga_tmp", [P, 3])
        woa, boa = sb("woa", [P, D]), sb("boa", [P, D])
        wk, wo, bv = sb("wk", [P, H // 2, D]), sb("wo", [P, H // 2, D]), sb("bv", [P, H // 2])
        wq1, wv1, bq1 = sb("wq1", [P, H // 2, 2, D]), sb("wv1", [P, H // 2, 2, D]), sb("bq1", [P, 2, H // 2])
        bo = sb("bo", [P, 1])
        m_hi, m_lo = sb("m_hi", [P, H, D], F32R), sb("m_lo", [P, H, D], F32R)
        wvo_hi, wvo_lo = sb("wvo_hi", [P, H, D], F32R), sb("wvo_lo", [P, H, D], F32R)
        u_bias, o_bias = sb("u_bias", [P, H]), sb("o_bias", [P, 1])
        wg_i, wu_i, wd_i = sb("wg_i", [P, F], I32), sb("wu_i", [P, F], I32), sb("wd_i", [P, FC, D], I32)
        wg, wu, wd = sb("wg", [P, F], F32R), sb("wu", [P, F], F32R), sb("wd", [P, FC, D])
        ident = sb("ident", [P, P])
        mask = sb("mask", [P, N])
        mean_w = sb("mean_w", [P, P])
        minus_half = sb("minus_half", [P, TILES])

        x = sb("x", [P, PAIRS * TILES, D])
        stats, mv, var, rstd = sb("stats", [P, TILES, 6]), sb("mv", [P, TILES, 2]), sb("var", [P, TILES]), sb("rstd", [P, TILES])
        xn = sb("xn", [P, TILES, D])
        xt_hi, xt_lo = sb("xt_hi", [P, PAIR], F32R), sb("xt_lo", [P, PAIR], F32R)
        rt_hi, rt_lo, rt = sb("rt_hi", [P, PAIR], F32R), sb("rt_lo", [P, PAIR], F32R), sb("rt", [P, PAIR])
        t_qkv = sb("t_qkv", [P, 3, PAIR])
        sv, tq, ntk, vwo = sb("sv", [P, PAIR]), sb("tq", [P, PAIR]), sb("ntk", [P, TILES]), sb("vwo", [P, TILES, D])
        dist, expd, less, signed, stdp = (sb(n, [P, TILES, N]) for n in ("dist", "expd", "less", "signed", "stdp"))
        xb = sb("xb", [P, TILES, D])
        gate_t, gated, hid = sb("gate_t", [P, PAIR]), sb("gated", [P, PAIR]), sb("hid", [P, FC, PAIR])
        u = sb("u", [P, 2, PAIR])
        v = sb("v", [P, 2, TILES, GH * D])
        neg_s = sb("neg_s", [P, 2, SC])
        neg_max, row_sum, row_inv = sb("neg_max", [P, 4, 2]), sb("row_sum", [P, 4, 2]), sb("row_inv", [P, 4, 2])
        prob = sb("prob", [P, 4, SC])
        prob_t = sb("prob_t", [P, 2, SC])
        o_t = sb("o_t", [P, PAIR])

        bank = [ctx.enter_context(nc.psum_tensor(f"bank{i}", [P, 512], F32)) for i in range(8)]
        s_ps, pt_ps, u_ps, v_ps, o_ps, X, Y = bank[0:2], bank[2], bank[3], bank[4], bank[5], bank[6], bank[7]

        ld_x0, ld_x, ld_a, ld_f, ld_v, ld_q = (sem(n) for n in ("ld_x0", "ld_x", "ld_a", "ld_f", "ld_v", "ld_q"))
        zeros = sem("zeros")
        consts = sem("consts")
        consts_in = sem("consts_in")
        wa_ready, ga_v, ga_pow, ga_ready, wf_ready = sem("wa_ready"), sem("ga_v"), sem("ga_pow"), sem("ga_ready"), sem("wf_ready")
        w_full, w_hi, w_lo = sem("w_full"), sem("w_hi"), sem("w_lo")
        link_s = sem("link")
        ln_var, ln_rstd, xn_ready = sem("ln_var"), sem("ln_rstd"), sem("xn_ready")
        xt_hi_s = sem("xt_hi_s")
        x_full, x_free, y_full, y_free = sem("x_full"), sem("x_free"), sem("y_full"), sem("y_free")
        sv_s, less_s, dist_s, exp_s, sign_s, stdp_s, xb_s = (sem(n) for n in ("sv_s", "less_s", "dist_s", "exp_s", "sign_s", "stdp_s", "xb_s"))
        gate_s, rt_hi_s = sem("gate_s"), sem("rt_hi_s")
        u_full, u_sb, v_full, v_sb = sem("u_full"), sem("u_sb"), sem("v_full"), sem("v_sb")
        s_full, s_masked, p_exp, p_inv, p_norm = sem("s_full"), sem("s_masked"), sem("p_exp"), sem("p_inv"), sem("p_norm")
        pt_full, pt_sb, pv_done, o_sb = sem("pt_full"), sem("pt_sb"), sem("pv_done"), sem("o_sb")
        stored = sem("stored")

        chunks_at = {-1: [0, 1], 0: [2], 1: [3], **{2 * c - 5: [c] for c in range(TILES, CH)}}

        def v_bank(c):
            return s_ps[1] if c == 1 else v_ps

        def pairs(side, main, lag=0):
            at = Tally()
            for job, p in PROLOGUE:
                side(job, p, at)
                at.passed(job)
            for p in range(PAIRS):
                for step in range(-1, STEPS + 3 + lag):
                    main(p, step, at)
                    for job, off in BODY.get(step - lag, []):
                        if 0 <= p + off < PAIRS and not (p == 0 and step - lag in A_STEPS):
                            side(job, p + off, at)
                            at.passed(job)
            for job in EPILOGUE:
                side(job, PAIRS - 1, at)
                at.passed(job)

        block = ctx.enter_context(nc.Block())

        @block.sync
        def _(sp):
            sp.dma_start(x[:, 0:TILES, :], x_view[:, 0:TILES, :]).then_inc(ld_x0, 16)
            sp.dma_start(wo[:], wo_d).then_inc(ld_v, 16)
            for dst, src in ((ga, ga_d), (wa, wa_d), (woa, woa_d), (boa, boa_d)):
                sp.dma_start(dst[:], src).then_inc(ld_a, 16)
            for p in range(1, PAIRS):
                sp.dma_start(x[:, p * TILES:(p + 1) * TILES, :], x_view[:, p * TILES:(p + 1) * TILES, :]).then_inc(ld_x, 16)
            for dst, src in ((wg_i, wg_d), (wu_i, wu_d), (wd_i, wd_d)):
                sp.dma_start(dst[:], src).then_inc(ld_f, 16)

            def side(job, p, at):
                if job == "down" and at.o == p + 1:
                    sp.wait_ge(x_free, at.x + 1)
                    ts = bass.ds(p * TILES, TILES)
                    sp.dma_start(out_view[:, ts, :], x[:, ts, :]).then_inc(stored, 16)

            pairs(side, lambda p, step, at: None)
            sp.wait_ge(stored, 16 * PAIRS)

        @block.tensor
        def _(pe):
            def split3(out, w_hi_ap, w_lo_ap, r_hi_ap, r_lo_ap):
                nc.tensor.matmul(out, w_hi_ap, r_hi_ap, start=True, stop=False)
                nc.tensor.matmul(out, w_lo_ap, r_hi_ap, start=False, stop=False)
                return nc.tensor.matmul(out, w_hi_ap, r_lo_ap, start=False, stop=True)

            def use_x(at):
                if isinstance(at.x, int) and at.x == 0:
                    return
                pe.wait_ge(x_free, at.x)

            def use_y(at):
                if isinstance(at.y, int) and at.y == 0:
                    return
                pe.wait_ge(y_free, at.y)

            def side(job, p, at):
                if job in ("lntA", "lntF", "lntB"):
                    if at.ln == 1:
                        pe.wait_ge(consts, 1)
                    pe.wait_ge(xn_ready, at.ln)
                    use_x(at)
                    for j in range(TILES):
                        last = nc.tensor.transpose(X[:, j * P:(j + 1) * P], xn[:, j, :], ident[:])
                    last.then_inc(x_full, 1)
                    if job != "lntB":
                        pass
                elif job.startswith("qkv"):
                    w = int(job[3])
                    if w == 0:
                        pe.wait_ge(wa_ready, 1)
                        pe.wait_ge(x_free, at.x)
                    if w == 1:
                        use_x(at)
                        split3(X[:], wa_hi[:, w, :], wa_lo[:, w, :], xt_hi[:], xt_lo[:]).then_inc(x_full, 1)
                    else:
                        use_y(at)
                        split3(Y[:], wa_hi[:, w, :], wa_lo[:, w, :], xt_hi[:], xt_lo[:]).then_inc(y_full, 1)
                elif job == "mean":
                    use_x(at)
                    use_y(at)
                    nc.tensor.matmul(X[:], mean_w[:], t_qkv[:, 0, :], start=True, stop=True).then_inc(x_full, 1)
                    for j in range(TILES):
                        last = nc.tensor.matmul(Y[:, j:j + 1], t_qkv[:, 1, j * P:(j + 1) * P], mean_w[:, 0:1], start=True, stop=True)
                    last.then_inc(y_full, 1)
                elif job == "vwo":
                    pe.wait_ge(sv_s, at.a + 1)
                    use_x(at)
                    for j in range(TILES):
                        last = nc.tensor.matmul(X[:, j * D:(j + 1) * D], sv[:, j * P:(j + 1) * P], woa[:], start=True, stop=True)
                    last.then_inc(x_full, 1)
                elif job == "aout":
                    pe.wait_ge(x_free, at.x)
                    pe.wait_ge(stdp_s, at.a + 1)
                    use_y(at)
                    for q in range(TILES):
                        b, qt = divmod(q, 2)
                        for kt in range(2):
                            last = nc.tensor.matmul(Y[:, q * D:(q + 1) * D], stdp[:, 2 * b + kt, qt * P:(qt + 1) * P],
                                                    vwo[:, 2 * b + kt, :], start=(kt == 0), stop=(kt == 1))
                    last.then_inc(y_full, 1)
                elif job.startswith("gu"):
                    c = int(job[2])
                    if c == 0:
                        pe.wait_ge(wf_ready, 1)
                        pe.wait_ge(x_free, at.x)
                    cs = slice(c * P, (c + 1) * P)
                    use_x(at)
                    nc.tensor.matmul(X[:], wg[:, cs], xt_hi[:], start=True, stop=False)
                    nc.tensor.matmul(X[:], wg[:, cs], xt_lo[:], start=False, stop=True).then_inc(x_full, 1)
                    use_y(at)
                    nc.tensor.matmul(Y[:], wu[:, cs], xt_hi[:], start=True, stop=False)
                    nc.tensor.matmul(Y[:], wu[:, cs], xt_lo[:], start=False, stop=True).then_inc(y_full, 1)
                elif job == "down":
                    pe.wait_ge(y_free, at.y)
                    use_x(at)
                    for j in range(TILES):
                        for c in range(FC):
                            last = nc.tensor.matmul(X[:, j * D:(j + 1) * D], hid[:, c, j * P:(j + 1) * P], wd[:, c, :],
                                                    start=(c == 0), stop=(c == FC - 1))
                    last.then_inc(x_full, 1)
                elif job == "bout":
                    pe.wait_ge(o_sb, at.o + 1)
                    use_x(at)
                    for j in range(TILES):
                        last = nc.tensor.transpose(X[:, j * P:(j + 1) * P], o_t[:, j * P:(j + 1) * P], ident[:])
                    last.then_inc(x_full, 1)
                elif job == "wb":
                    pe.wait_ge(w_lo, 8)
                    for i in range(H // 2):
                        nc.tensor.matmul(v_ps[:, 2 * i:2 * i + 2], wk[:, i, :], bq1[:, :, i], start=True, stop=True)
                    for i in range(H // 2):
                        last = nc.tensor.matmul(v_ps[:, H:H + 1], wo[:, i, :], bv[:, i:i + 1], start=(i == 0), stop=(i == H // 2 - 1))
                    last.then_inc(w_full, 1)
                elif job in WEIGHTS:
                    i = int(job[1])
                    if i == 0:
                        pe.wait_ge(ld_v, 16 * 3)
                    if i == 4:
                        pe.wait_ge(ld_q, 16 * 7)
                    if i >= 2:
                        pe.wait_ge(w_lo, i - 1)
                    left, right = (wv1, wo) if i < 4 else (wq1, wk)
                    for j in range(4):
                        h = 4 * (i % 4) + j
                        last = nc.tensor.matmul((u_ps, v_ps)[i % 2][:, j * D:(j + 1) * D], left[:, h // 2, h % 2, :], right[:, h // 2, :], start=True, stop=True)
                    last.then_inc(w_full, 1)

            def u_proj(p, h, at):
                if h == 0:
                    pe.wait_ge(rt_hi_s, p + 1)
                    pe.wait_ge(x_free, at.x)
                if not (isinstance(p, int) and p == 0 and h == 0):
                    pe.wait_ge(u_sb, H * p + h)
                split3(u_ps[:], m_hi[:, h, :], m_lo[:, h, :], rt_hi[:], rt_lo[:]).then_inc(u_full, 1)

            def v_proj(p, c):
                g, j = divmod(c, TILES)
                if c == 1 and not (isinstance(p, int) and p == 0):
                    pe.wait_ge(s_masked, STEPS * p)
                elif c > 1:
                    pe.wait_ge(v_sb, CH * p + max(c, 2) - (c == 2))
                elif c == 0 and not (isinstance(p, int) and p == 0):
                    pe.wait_ge(v_sb, CH * p)
                hs = slice(GH * g, GH * (g + 1))
                js = slice(j * P, (j + 1) * P)
                split3(v_bank(c)[:], rt_hi[:, js], rt_lo[:, js], wvo_hi[:, hs, :], wvo_lo[:, hs, :]).then_inc(v_full, 1)

            def main(p, step, at):
                if step == -1:
                    if p == 0:
                        pe.wait_ge(w_hi, 9)
                        pe.wait_ge(w_lo, 8)
                    u_proj(p, 0, at)
                    for c in chunks_at[-1]:
                        v_proj(p, c)
                    return
                if step < STEPS:
                    h, b = divmod(step, 2)
                    n = STEPS * p + step
                    pe.wait_ge(u_sb, H * p + h + 1)
                    if step == 1:
                        pe.wait_ge(v_sb, CH * p + 2)
                    elif not (isinstance(p, int) and n < 2):
                        pe.wait_ge(s_masked, n - 1)
                    S, t = s_ps[step % 2], b * N
                    nc.tensor.matmul(S[:, 0:P], u[:, h % 2, t:t + P], rt[:, t:t + P], start=True, stop=True)
                    nc.tensor.matmul(S[:, P:SC], u[:, h % 2, t + P:t + N], rt[:, t:t + N], start=True, stop=True).then_inc(s_full, 1)
                if 2 <= step < STEPS + 2:
                    k = step - 2
                    n = STEPS * p + k
                    pe.wait_ge(p_norm, n + 1)
                    if not (isinstance(p, int) and n == 0):
                        pe.wait_ge(pt_sb, n)
                    for j in range(3):
                        last = nc.tensor.transpose(pt_ps[:, j * P:(j + 1) * P], prob[:, k % 4, j * P:(j + 1) * P], ident[:])
                    last.then_inc(pt_full, 1)
                if step >= 3:
                    k = step - 3
                    h, b = divmod(k, 2)
                    n = STEPS * p + k
                    pe.wait_ge(pt_sb, n + 1)
                    pe.wait_ge(v_sb, CH * p + TILES * (h // GH) + TILES)
                    if k == 0 and not (isinstance(p, int) and p == 0):
                        pe.wait_ge(o_sb, p)
                    hs = slice((h % GH) * D, (h % GH + 1) * D)
                    vg = v[:, (h // GH) % 2]
                    nc.tensor.matmul(o_ps[:, b * N:(b + 1) * N], vg[:, 2 * b, hs], prob_t[:, k % 2, 0:N],
                                     start=(k == 0), stop=False, skip_group_check=True)
                    nc.tensor.matmul(o_ps[:, b * N + P:(b + 1) * N], vg[:, 2 * b + 1, hs], prob_t[:, k % 2, N:SC],
                                     start=False, stop=(k >= STEPS - 2), skip_group_check=True).then_inc(pv_done, 1)
                if step < STEPS and step % 2 == 0 and step // 2 + 1 < H:
                    u_proj(p, step // 2 + 1, at)
                for c in chunks_at.get(step, []):
                    v_proj(p, c)

            pairs(side, main)

        @block.scalar
        def _(act):
            act.wait_ge(zeros, 1)
            for i in range(2):
                half = slice(i * A, (i + 1) * A)
                act.dma_start(wv1[half, :, i, :], wv_d[half, :, :]).then_inc(ld_v, 16)
            act.dma_start(wk[:], wk_d).then_inc(ld_q, 16)
            act.wait_ge(zeros, 3)
            for i in range(2):
                half = slice(i * A, (i + 1) * A)
                act.dma_start(wq1[half, :, i, :], wq_d[half, :, :]).then_inc(ld_q, 16)
                act.dma_start(bq1[half, i, :], bq_d[half, :]).then_inc(ld_q, 16)
            act.dma_start(bv[:], bv_d).then_inc(ld_q, 16)
            act.dma_start(bo[:], bo_d).then_inc(ld_q, 16)

            def side(job, p, at):
                if job in ("lntA", "lntF"):
                    act.wait_ge(x_full, at.x + 1)
                    if at.xt:
                        act.wait_ge(y_full, at.y)
                    nc.scalar.activation(xt_hi[:], X[:], ACT.Copy).then_inc(xt_hi_s, 1)
                elif job == "lntB":
                    act.wait_ge(x_full, at.x + 1)
                    if not (isinstance(p, int) and p == 0):
                        act.wait_ge(u_full, H * p)
                        act.wait_ge(v_full, CH * p)
                        act.wait_ge(s_full, STEPS * p)
                    nc.scalar.activation(rt[:], X[:], ACT.Copy)
                    nc.scalar.activation(rt_hi[:], X[:], ACT.Copy).then_inc(rt_hi_s, 1)
                elif job.startswith("qkv"):
                    w = int(job[3])
                    if at.a == 0 and w == 0:
                        act.wait_ge(ga_ready, 1)
                    if w == 1:
                        act.wait_ge(x_full, at.x + 1)
                        nc.scalar.activation(t_qkv[:, w, :], X[:], ACT.Tanh, bias=ga_bias[:, w:w + 1],
                                             scale=ga_scale[:, w:w + 1]).then_inc(x_free, 1)
                    else:
                        act.wait_ge(y_full, at.y + 1)
                        if w == 2 and at.a:
                            act.wait_ge(sv_s, at.a)
                        nc.scalar.activation(t_qkv[:, w, :], Y[:], ACT.Tanh, bias=ga_bias[:, w:w + 1],
                                             scale=ga_scale[:, w:w + 1]).then_inc(y_free, 1)
                elif job == "mean":
                    pass
                elif job == "vwo":
                    act.wait_ge(x_full, at.x + 1)
                    nc.scalar.activation(vwo[:], X[:].rearrange("p (j d) -> p j d", d=D), ACT.Copy).then_inc(x_free, 1)
                elif job == "mat0":
                    act.wait_ge(x_free, at.x - 1)
                    act.wait_ge(y_free, at.y)
                    for j in range(TILES):
                        b = j // 2
                        last = nc.scalar.activation(dist[:, j, :], tq[:, b * N:(b + 1) * N], ACT.Abs, bias=ntk[:, j:j + 1])
                    last.then_inc(dist_s, 1)
                    act.wait_ge(dist_s, at.a + 1)
                    nc.scalar.activation(expd[:], dist[:], ACT.Exp, scale=-INV_TAU).then_inc(exp_s, 1)
                elif job == "aout":
                    pass
                elif job.startswith("gu"):
                    c = int(job[2])
                    act.wait_ge(x_full, at.x + 1)
                    act.wait_ge(x_free, at.x)
                    nc.scalar.activation(gate_t[:], X[:], ACT.Tanh, scale=0.5 * W_SCALE).then_inc(gate_s, 1)
                elif job == "down":
                    pass
                elif job == "bout":
                    pass
                elif job == "wb":
                    act.wait_ge(w_full, 9)
                    nc.scalar.activation(u_bias[:], v_ps[:, 0:H], ACT.Copy, scale=SCORE_SCALE)
                    nc.scalar.activation(o_bias[:], v_ps[:, H:H + 1], ACT.Identity, bias=bo[:]).then_inc(w_hi, 1)
                elif job in WEIGHTS:
                    i = int(job[1])
                    act.wait_ge(w_full, i + 1)
                    dst = (wvo_hi, m_hi)[i // 4][:, 4 * (i % 4):4 * (i % 4) + 4, :]
                    nc.scalar.activation(dst, (u_ps, v_ps)[i % 2][:].rearrange("p (j d) -> p j d", d=D), ACT.Copy,
                                         scale=(1.0, SCORE_SCALE)[i // 4]).then_inc(w_hi, 1)

            def u_evac(p, h):
                act.wait_ge(u_full, H * p + h + 1)
                if not (isinstance(p, int) and p == 0 and h < 2):
                    act.wait_ge(s_full, STEPS * p + 2 * h - 2)
                nc.scalar.activation(u[:, h % 2, :], u_ps[:], ACT.Identity, bias=u_bias[:, h:h + 1]).then_inc(u_sb, 1)

            def v_evac(p, c):
                g, j = divmod(c, TILES)
                act.wait_ge(v_full, CH * p + c + 1)
                if not (isinstance(p, int) and p == 0 and g < 2):
                    act.wait_ge(pv_done, STEPS * p + 2 * GH * (g - 1))
                nc.scalar.activation(v[:, g % 2, j, :], v_bank(c)[:], ACT.Copy).then_inc(v_sb, 1)

            def exp(p, k):
                n = STEPS * p + k
                act.wait_ge(s_masked, n + 1)
                if not (isinstance(p, int) and n < 4):
                    act.wait_ge(pt_full, n - 3)
                    act.wait_ge(p_inv, n - 3)
                q, r = k % 4, k % 2
                nc.scalar.activation(prob[:, q, 0:P], neg_s[:, r, 0:P], ACT.Exp, bias=neg_max[:, q, 0:1], scale=-1.0,
                                     accum_out=row_sum[:, q, 0:1])
                nc.scalar.activation(prob[:, q, P:SC], neg_s[:, r, P:SC], ACT.Exp, bias=neg_max[:, q, 1:2], scale=-1.0,
                                     accum_out=row_sum[:, q, 1:2]).then_inc(p_exp, 1)

            def main(p, step, at):
                if step == -1:
                    u_evac(p, 0)
                    for c in chunks_at[-1]:
                        v_evac(p, c)
                    return
                if 2 <= step < STEPS + 2:
                    k = step - 2
                    n = STEPS * p + k
                    act.wait_ge(pt_full, n + 1)
                    if not (isinstance(p, int) and n < 2):
                        act.wait_ge(pv_done, n - 1)
                    nc.scalar.activation(prob_t[:, k % 2, :], pt_ps[:, 0:SC], ACT.Copy).then_inc(pt_sb, 1)
                if step < STEPS:
                    exp(p, step)
                if step % 2 == 0 and step // 2 + 1 < H:
                    u_evac(p, step // 2 + 1)
                for c in chunks_at.get(step, []):
                    v_evac(p, c)
                if step == STEPS + 2:
                    act.wait_ge(pv_done, STEPS * (p + 1))
                    act.wait_ge(x_full, at.x)
                    nc.scalar.activation(o_t[:], o_ps[:], ACT.Identity, bias=o_bias[:]).then_inc(o_sb, 1)

            pairs(side, main)

        @block.vector
        def _(dve):
            def link(ins, at):
                ins.then_inc(link_s, 1)
                at.link += 1
                dve.wait_ge(link_s, at.link)

            def side(job, p, at):
                if job == "lns0":
                    if at.ln == 0:
                        dve.wait_ge(ld_x0, 16)
                    else:
                        if p == 1 and at.ln == 1:
                            dve.wait_ge(ld_x, 16 * (PAIRS - 1))
                        dve.wait_ge(x_free, at.x)
                        if at.y:
                            dve.wait_ge(y_free, at.y)
                    for j in range(TILES):
                        last = nc.vector.bn_stats(stats[:, j, :], x[:, bass.ds(p * TILES + j, 1), :].rearrange("p o d -> p (o d)"))
                    link(last, at)
                    for j in range(TILES):
                        last = nc.vector.bn_aggr(mv[:, j, :], stats[:, j, :])
                    link(last, at)
                    nc.vector.tensor_scalar(var[:], mv[:, :, 1], EPS, None, ALU.add).then_inc(ln_var, 1)
                    if at.ln == 0:
                        dve.wait_ge(ld_a, 64)
                        link(nc.vector.tensor_copy(wa_hi[:], wa[:]), at)
                        nc.vector.tensor_tensor(wa_lo[:], wa[:], wa_hi[:].bitcast(F32), ALU.subtract).then_inc(wa_ready, 1)
                elif job == "lns1":
                    dve.wait_ge(ln_rstd, at.ln + 1)
                    if at.ln:
                        dve.wait_ge(x_full, at.x)
                    for j in range(TILES):
                        last = nc.vector.tensor_scalar(xn[:, j, :], x[:, bass.ds(p * TILES + j, 1), :].rearrange("p o d -> p (o d)"),
                                                       mv[:, j, 0:1], rstd[:, j:j + 1], ALU.subtract, ALU.mult)
                    last.then_inc(xn_ready, 1)
                    if at.ln == 0:
                        nc.vector.tensor_scalar(ga_tmp[:], ga[:, 3, :], EPS, None, ALU.add).then_inc(ga_v, 1)
                        dve.wait_ge(ga_pow, 1)
                        link(nc.vector.scalar_tensor_tensor(ga_scale[:], ga_rs[:], 2.0, ga[:, 0, :], ALU.mult, ALU.mult), at)
                        link(nc.vector.tensor_tensor(ga_tmp[:], ga[:, 2, :], ga_scale[:], ALU.mult), at)
                        link(nc.vector.scalar_tensor_tensor(ga_bias[:], ga[:, 1, :], 2.0, ga_tmp[:], ALU.mult, ALU.subtract), at)
                        nc.vector.tensor_scalar(ga_bias[:], ga_bias[:], -2.0, None, ALU.add).then_inc(ga_ready, 1)
                elif job in ("lntA", "lntF"):
                    dve.wait_ge(xt_hi_s, at.xt + 1)
                    nc.vector.tensor_tensor(xt_lo[:], X[:], xt_hi[:].bitcast(F32), ALU.subtract).then_inc(x_free, 1)
                elif job == "lntB":
                    dve.wait_ge(rt_hi_s, p + 1)
                    nc.vector.tensor_tensor(rt_lo[:], X[:], rt_hi[:].bitcast(F32), ALU.subtract).then_inc(x_free, 1)
                elif job.startswith("qkv"):
                    if at.a == 0 and job == "qkv2":
                        dve.wait_ge(ld_f, 48)
                        nc.vector.tensor_copy(wg[:], wg_i[:])
                        nc.vector.tensor_copy(wu[:], wu_i[:])
                        nc.vector.tensor_copy(wd[:], wd_i[:]).then_inc(wf_ready, 1)
                elif job == "mean":
                    dve.wait_ge(x_full, at.x + 1)
                    nc.vector.tensor_scalar(tq[:], X[:], 0.5, None, ALU.add).then_inc(x_free, 1)
                    dve.wait_ge(y_full, at.y + 1)
                    nc.vector.tensor_scalar(ntk[:], Y[:, 0:TILES], 0.5, -1.0, ALU.add, ALU.mult).then_inc(y_free, 1)
                elif job == "vwo":
                    pass
                elif job == "mat0":
                    dve.wait_ge(x_free, at.x - 1)
                    dve.wait_ge(y_free, at.y)
                    for j in range(TILES):
                        b = j // 2
                        last = nc.vector.tensor_scalar(less[:, j, :], tq[:, b * N:(b + 1) * N], ntk[:, j:j + 1], 0.0, ALU.add, ALU.is_lt)
                    last.then_inc(less_s, 1)
                elif job == "mat1":
                    dve.wait_ge(less_s, at.a + 1)
                    dve.wait_ge(exp_s, at.a + 1)
                    nc.vector.scalar_tensor_tensor(signed[:], less[:], -0.5, expd[:], ALU.add, ALU.mult).then_inc(sign_s, 1)
                elif job == "aout":
                    dve.wait_ge(y_full, at.y + 1)
                    dve.wait_ge(xb_s, at.a + 1)
                    nc.vector.tensor_tensor(x[:, bass.ds(p * TILES, TILES), :], Y[:].rearrange("p (j d) -> p j d", d=D), xb[:], ALU.add).then_inc(y_free, 1)
                elif job.startswith("gu"):
                    c = int(job[2])
                    dve.wait_ge(gate_s, FC * at.f + c + 1)
                    if at.y:
                        dve.wait_ge(y_free, at.y)
                    nc.vector.scalar_tensor_tensor(gated[:], gate_t[:], 1.0, X[:], ALU.add, ALU.mult).then_inc(x_free, 1)
                    dve.wait_ge(x_free, at.x + 1)
                    dve.wait_ge(y_full, at.y + 1)
                    nc.vector.tensor_tensor(hid[:, c, :], gated[:], Y[:], ALU.mult).then_inc(y_free, 1)
                elif job == "down":
                    dve.wait_ge(x_full, at.x + 1)
                    xs = x[:, bass.ds(p * TILES, TILES), :]
                    nc.vector.scalar_tensor_tensor(xs, X[:].rearrange("p (j d) -> p j d", d=D), 0.5 * W_SCALE ** 3, xs,
                                                   ALU.mult, ALU.add).then_inc(x_free, 1)
                elif job == "bout":
                    dve.wait_ge(x_full, at.x + 1)
                    xs = x[:, bass.ds(p * TILES, TILES), :]
                    nc.vector.tensor_tensor(xs, X[:].rearrange("p (j d) -> p j d", d=D), xs, ALU.add).then_inc(x_free, 1)
                elif job == "wb":
                    pass
                elif job in WEIGHTS:
                    i = int(job[1])
                    dve.wait_ge(w_hi, i + 1)
                    hs = slice(4 * (i % 4), 4 * (i % 4) + 4)
                    hi, lo = ((wvo_hi, wvo_lo), (m_hi, m_lo))[i // 4]
                    nc.vector.scalar_tensor_tensor(lo[:, hs, :], (u_ps, v_ps)[i % 2][:].rearrange("p (j d) -> p j d", d=D),
                                                   (1.0, SCORE_SCALE)[i // 4], hi[:, hs, :].bitcast(F32), ALU.mult, ALU.subtract).then_inc(w_lo, 1)

            def main(p, step, at):
                if step == 0 and isinstance(p, int) and p == 0:
                    dve.wait_ge(consts, 2)
                if 0 <= step < STEPS:
                    n = STEPS * p + step
                    dve.wait_ge(s_full, n + 1)
                    if not (isinstance(p, int) and n < 2):
                        dve.wait_ge(p_exp, n - 1)
                    r, q = step % 2, step % 4
                    nc.vector.tensor_tensor_reduce(out=neg_s[:, r, 0:P], in0=s_ps[r][:, 0:P], in1=mask[:, P:N], scale=-1.0, scalar=3e38,
                                                   op0=ALU.add, op1=ALU.min, accum_out=neg_max[:, q, 0:1])
                    nc.vector.tensor_tensor_reduce(out=neg_s[:, r, P:SC], in0=s_ps[r][:, P:SC], in1=mask[:], scale=-1.0, scalar=3e38,
                                                   op0=ALU.add, op1=ALU.min, accum_out=neg_max[:, q, 1:2]).then_inc(s_masked, 1)
                if 1 <= step < STEPS + 1:
                    k = step - 1
                    dve.wait_ge(p_exp, STEPS * p + k + 1)
                    q = k % 4
                    nc.vector.reciprocal(row_inv[:, q, :], row_sum[:, q, :]).then_inc(p_inv, 1)
                    dve.wait_ge(p_inv, STEPS * p + k + 1)
                    nc.vector.tensor_scalar(prob[:, q, 0:P], prob[:, q, 0:P], row_inv[:, q, 0:1], None, ALU.mult)
                    nc.vector.tensor_scalar(prob[:, q, P:SC], prob[:, q, P:SC], row_inv[:, q, 1:2], None, ALU.mult).then_inc(p_norm, 1)

            pairs(side, main)

        @block.gpsimd
        def _(pool):
            nc.gpsimd.memset(wv1[:], 0.0).then_inc(zeros, 1)
            nc.gpsimd.memset(wq1[:], 0.0).then_inc(zeros, 1)
            nc.gpsimd.memset(bq1[:], 0.0).then_inc(zeros, 1)
            nc.gpsimd.memset(ident[:], 0.0).then_inc(consts_in, 1)
            nc.gpsimd.memset(mask[:], 0.0).then_inc(consts_in, 1)
            nc.gpsimd.memset(mean_w[:], -0.5 / D).then_inc(consts_in, 1)
            nc.gpsimd.memset(minus_half[:], -0.5).then_inc(consts_in, 1)
            pool.wait_ge(consts_in, 4)
            nc.gpsimd.affine_select(out=ident[:], in_=ident[:], compare_op=ALU.not_equal, fill=1.0, base=0,
                                    pattern=[[-1, P]], channel_multiplier=1).then_inc(consts, 1)
            nc.gpsimd.affine_select(out=mask[:, P:N], in_=mask[:, P:N], compare_op=ALU.is_ge, fill=-BIG, base=0,
                                    pattern=[[-1, P]], channel_multiplier=1).then_inc(consts, 1)

            def side(job, p, at):
                if job == "lns0":
                    pool.wait_ge(ln_var, at.ln + 1)
                    nc.gpsimd.tensor_tensor(rstd[:], var[:], minus_half[:], ALU.pow).then_inc(ln_rstd, 1)
                elif job == "lns1" and at.ln == 0:
                    pool.wait_ge(ga_v, 1)
                    nc.gpsimd.tensor_tensor(ga_rs[:], ga_tmp[:], minus_half[:, 0:3], ALU.pow).then_inc(ga_pow, 1)
                elif job == "qkv2":
                    pool.wait_ge(y_free, at.y + 1)
                    nc.gpsimd.tensor_scalar(sv[:], t_qkv[:, 2, :], 0.5, 0.5, ALU.mult, ALU.add).then_inc(sv_s, 1)
                elif job == "mat0":
                    nc.gpsimd.tensor_tensor(xb[:], x[:, bass.ds(p * TILES, TILES), :], boa[:, :].unsqueeze(1).to_broadcast([P, TILES, D]), ALU.add).then_inc(xb_s, 1)
                elif job == "mat1":
                    pool.wait_ge(sign_s, at.a + 1)
                    nc.gpsimd.tensor_scalar(stdp[:], signed[:], 2.0 * A_STDP, W_OFF, ALU.mult, ALU.add).then_inc(stdp_s, 1)

            pairs(side, lambda p, step, at: None)


def kernel(**inputs):
    import numpy as np
    import concourse.bacc as bacc
    from concourse.bass_utils import run_bass_kernel_spmd

    a = {k.removeprefix("L0_"): np.asarray(v) for k, v in inputs.items()}
    x = a["attn_a_x"]

    def head_pairs(w):
        return w.reshape(H // 2, P, D).transpose(1, 0, 2)

    arrays = {
        "x": x.reshape(B * N, D),
        "wa": np.stack([a[f"attn_a_W{c}"] for c in "qkv"], 1),
        "ga": np.stack([np.stack([a[f"attn_a_{n}{c}"] for c in "qkv"], 1) for n in "gbmv"], 1),
        "woa": a["attn_a_Wo"],
        "boa": np.tile(a["attn_a_bo"][None, :], (P, 1)),
        "wq": head_pairs(a["attn_b_Wq"].transpose(0, 2, 1)),
        "wk": head_pairs(a["attn_b_Wk"].transpose(0, 2, 1)),
        "wv": head_pairs(a["attn_b_Wv"].transpose(0, 2, 1)),
        "wo": head_pairs(a["attn_b_Wo"]),
        "bq": a["attn_b_bq"].reshape(H // 2, P).T,
        "bv": a["attn_b_bv"].reshape(H // 2, P).T,
        "bo": a["attn_b_bo"][:, None],
        "wg": a["ffn_w_gate"].T,
        "wu": a["ffn_w_up"].T,
        "wd": a["ffn_w_down"].T.reshape(FC, P, D).transpose(1, 0, 2),
    }
    arrays = {f"{k}_in": np.ascontiguousarray(v) for k, v in arrays.items()}
    nc = bacc.Bacc("TRN2", target_bir_lowering=False, num_devices=1)
    args = [nc.dram_tensor(k, v.shape, mybir.dt.from_np(v.dtype), kind="ExternalInput").ap() for k, v in arrays.items()]
    out = nc.dram_tensor("out", (B * N, D), F32, kind="ExternalOutput").ap()
    build(nc, *args, out)
    r = run_bass_kernel_spmd(nc, [arrays], core_ids=[0])
    return r.results[0]["out"].reshape(x.shape)
```

```python
from contextlib import ExitStack

import concourse.bass as bass
from concourse import mybir

P = 128
ALU = mybir.AluOpType
ACT = mybir.ActivationFunctionType
F32 = mybir.dt.float32
F32R = mybir.dt.float32r
I32 = mybir.dt.int32

B, N, D = 8, 256, 128
H, A = 16, 64
F = 384
PAIR = 2 * N
PAIRS = B * N // PAIR
TILES = PAIR // P
FC = F // P
STEPS = 2 * H
GH = PAIR // D
GROUPS = H // GH
CH = GROUPS * TILES
SC = N + P
EPS = 1e-5
W_SCALE = 1.0 / 127.0
SCORE_SCALE = A ** -0.5
A_STDP, W_OFF, INV_TAU = 0.9, 0.9, 2.0
BIG = 1e30

BODY = {
    1: [("lns0", 1)], 3: [("lns1", 1)], 4: [("lntA", 1)], 5: [("qkv0", 1), ("qkv1", 1)], 6: [("qkv2", 1)], 7: [("mean", 1)],
    8: [("bout", -1)], 9: [("lns0", -1)], 10: [("vwo", 1), ("lns1", -1)], 11: [("lntF", -1), ("mat0", 1)], 12: [("mat1", 1)],
    13: [("gu0", -1)], 15: [("aout", 1), ("gu1", -1)], 17: [("lns0", 1), ("gu2", -1)], 18: [("lns1", 1)],
    19: [("down", -1), ("lntF", 1)], 20: [("gu0", 1)], 21: [("gu1", 1)], 22: [("gu2", 1)], 23: [("down", 1)],
    24: [("lns0", 1)], 25: [("lns1", 1)], 26: [("lntB", 1)],
}
U_AHEAD, V_AHEAD = 3, 4
T_LAG, PV_LAG = 3, 4
PROLOGUE = [
    ("lns0", 0, 2), ("lns1", 0, 2), ("lns0", 2, 2), ("lns1", 2, 2), ("lntA", 0, 2), ("w0", 0, 0), ("qkv0", 0, 2),
    ("lntA", 2, 2), ("w1", 0, 0), ("qkv1", 0, 2), ("qkv0", 2, 2), ("qkv1", 2, 2), ("qkv2", 0, 2), ("mean", 0, 2), ("w2", 0, 0),
    ("vwo", 0, 2), ("qkv2", 2, 2), ("mat0", 0, 2), ("mean", 2, 2), ("mat1", 0, 2), ("w3", 0, 0), ("vwo", 2, 2), ("mat0", 2, 2),
    ("aout", 0, 2), ("mat1", 2, 2), ("w4", 0, 0), ("lns0", 0, 2), ("lns1", 0, 2), ("aout", 2, 2), ("lns0", 2, 2),
    ("lntF", 0, 2), ("gu0", 0, 2), ("lns1", 2, 2), ("w5", 0, 0), ("lntF", 2, 2), ("gu0", 2, 2), ("w6", 0, 0), ("gu1", 0, 2),
    ("w7", 0, 0), ("gu2", 0, 2), ("down", 0, 2), ("lns0", 0, 2), ("gu1", 2, 2), ("gu2", 2, 2), ("down", 2, 2), ("lns0", 2, 2),
    ("lns1", 0, 2), ("lns1", 2, 2), ("wb", 0, 0), ("lntB", 0, 2), ("lntB", 2, 2),
]
EPILOGUE = [
    ("bout", 12, 2), ("lns0", 12, 2), ("bout", 14, 2), ("lns1", 12, 2), ("lns0", 14, 2), ("lntF", 12, 2), ("lns1", 14, 2),
    ("gu0", 12, 2), ("gu1", 12, 2), ("lntF", 14, 2), ("gu0", 14, 2), ("gu1", 14, 2), ("gu2", 12, 2), ("gu2", 14, 2),
    ("down", 12, 2), ("down", 14, 2),
]

USES = {"lntA": (1, 0), "lntF": (1, 0), "lntB": (1, 0), "qkv0": (0, 1), "qkv1": (1, 0), "qkv2": (0, 1), "mean": (1, 1),
        "vwo": (1, 0), "aout": (0, 1), "gu0": (1, 1), "gu1": (1, 1), "gu2": (1, 1), "down": (1, 0), "bout": (1, 0)}
KINDS = {"lntA": "lnt", "lntF": "lnt", "lntB": "lnt", "gu0": "gu", "gu1": "gu", "gu2": "gu"}


WEIGHTS = [f"w{i}" for i in range(8)]


class Counts:

    def __init__(self, n, x, y):
        self.n, self.x, self.y = n, x, y


class Tally:

    def __init__(self):
        self.x = 0
        self.y = 0
        self.link = 0
        self.jobs = {}
        self.last = {}
        self.added = set()
        self.second = set()

    def n(self, name):
        return self.jobs.get(name, 0)

    def after(self, name, t0, nt):
        found = [self.last[name, t % TILES] for t in range(t0, t0 + nt) if (name, t % TILES) in self.last]
        return max(found, key=lambda c: c.n) if found else None

    def passed(self, job, t0, nt):
        uses_x, uses_y = USES.get(job, (0, 0))
        self.x += uses_x
        self.y += uses_y
        names = [job] + ([KINDS[job]] if job in KINDS else []) + ["xt"] * (job in ("lntA", "lntF")) + ["xt_read"] * (job in ("qkv2", "gu2")) \
            + ["add"] * (job in ("aout", "down", "bout"))
        for name in names:
            self.jobs[name] = self.n(name) + 1
            for t in range(t0, t0 + nt):
                self.last[name, t % TILES] = Counts(self.jobs[name], self.x, self.y)
        tiles = range(t0, t0 + nt)
        if "add" in names:
            self.added.update(tiles)
        if job == "bout":
            self.second.update(tiles)


def build(nc, x_d, wa_d, ga_d, woa_d, boa_d, wq_d, wk_d, wv_d, wo_d, bq_d, bv_d, bo_d, wg_d, wu_d, wd_d, out_d):
    x_view = x_d.rearrange("(t p) d -> p t d", p=P)
    out_view = out_d.rearrange("(t p) d -> p t d", p=P)

    with ExitStack() as ctx:
        def sb(name, shape, dt=F32):
            return ctx.enter_context(nc.sbuf_tensor(name, shape, dt))

        def sem(name):
            return ctx.enter_context(nc.semaphore(name))

        wa = sb("wa", [P, 3, D])
        wa_hi, wa_lo = sb("wa_hi", [P, 3, D], F32R), sb("wa_lo", [P, 3, D], F32R)
        ga = sb("ga", [P, 4, 3])
        ga_scale, ga_bias, ga_rs, ga_tmp = sb("ga_scale", [P, 3]), sb("ga_bias", [P, 3]), sb("ga_rs", [P, 3]), sb("ga_tmp", [P, 3])
        woa, boa = sb("woa", [P, D]), sb("boa", [P, D])
        wk, wo, bv = sb("wk", [P, H // 2, D]), sb("wo", [P, H // 2, D]), sb("bv", [P, H // 2])
        wq1, wv1, bq1 = sb("wq1", [P, H // 2, 2, D]), sb("wv1", [P, H // 2, 2, D]), sb("bq1", [P, 2, H // 2])
        bo = sb("bo", [P, 1])
        m_hi, m_lo = sb("m_hi", [P, H, D], F32R), sb("m_lo", [P, H, D], F32R)
        wvo_hi, wvo_lo = sb("wvo_hi", [P, H, D], F32R), sb("wvo_lo", [P, H, D], F32R)
        u_bias, o_bias = sb("u_bias", [P, H]), sb("o_bias", [P, 1])
        wg_i, wu_i, wd_i = sb("wg_i", [P, F], I32), sb("wu_i", [P, F], I32), sb("wd_i", [P, FC, D], I32)
        wg, wu, wd = sb("wg", [P, F], F32R), sb("wu", [P, F], F32R), sb("wd", [P, FC, D])
        ident = sb("ident", [P, P])
        mask = sb("mask", [P, N])
        mean_w = sb("mean_w", [P, P])
        minus_half = sb("minus_half", [P, TILES])
        warm = sb("warm", [P, 1])

        x = sb("x", [P, PAIRS * TILES, D])
        stats, mv, var, rstd = sb("stats", [P, TILES, 6]), sb("mv", [P, TILES, 2]), sb("var", [P, TILES]), sb("rstd", [P, TILES])
        xn = sb("xn", [P, TILES, D])
        xt_hi, xt_lo = sb("xt_hi", [P, PAIR], F32R), sb("xt_lo", [P, PAIR], F32R)
        rt_hi, rt_lo, rt = sb("rt_hi", [P, 2, PAIR], F32R), sb("rt_lo", [P, 2, PAIR], F32R), sb("rt", [P, 2, PAIR])
        t_qkv = sb("t_qkv", [P, 3, PAIR])
        sv, tq, ntk, vwo = sb("sv", [P, PAIR]), sb("tq", [P, PAIR]), sb("ntk", [P, TILES]), sb("vwo", [P, TILES, D])
        dist, expd, less, signed, stdp = (sb(n, [P, TILES, N]) for n in ("dist", "expd", "less", "signed", "stdp"))
        xb = sb("xb", [P, TILES, D])
        gate_t, gated, hid = sb("gate_t", [P, PAIR]), sb("gated", [P, PAIR]), sb("hid", [P, FC, PAIR])
        u = sb("u", [P, 2, 2, P])
        u_hi, u_lo = sb("u_hi", [P, 2, 2, P], F32R), sb("u_lo", [P, 2, 2, P], F32R)
        v = sb("v", [P, 2, TILES, GH * D])
        neg_s = sb("neg_s", [P, 2, SC])
        neg_max, row_sum, row_inv = sb("neg_max", [P, 4, 2]), sb("row_sum", [P, 4, 2]), sb("row_inv", [P, 4, 2])
        prob = sb("prob", [P, 4, SC])
        prob_t = sb("prob_t", [P, 2, SC])
        o_t = sb("o_t", [P, PAIR])

        bank = [ctx.enter_context(nc.psum_tensor(f"bank{i}", [P, 512], F32)) for i in range(8)]
        s_ps, pt_ps, u_ps, v_ps, o_ps, X, Y = bank[0:2], bank[2], bank[3], bank[4], bank[5], bank[6], bank[7]

        u_tiles = u_ps[:].rearrange("p (b t q) -> p b t q", b=2, t=2)

        ld_x0, ld_x1, ld_x, ld_o, ld_a, ld_f, ld_v, ld_q = (sem(n) for n in ("ld_x0", "ld_x1", "ld_x", "ld_o", "ld_a", "ld_f", "ld_v", "ld_q"))
        zeros_v, zeros_q = sem("zeros_v"), sem("zeros_q")
        consts = sem("consts")
        consts_in = sem("consts_in")
        wa_ready, ga_v, ga_pow, ga_ready, wf_ready = sem("wa_ready"), sem("ga_v"), sem("ga_pow"), sem("ga_ready"), sem("wf_ready")
        w_full, w_hi, w_lo = sem("w_full"), sem("w_hi"), sem("w_lo")
        link_s = sem("link")
        ln_var, ln_rstd, xn_ready = sem("ln_var"), sem("ln_rstd"), sem("xn_ready")
        xt_hi_s = sem("xt_hi_s")
        x_full, x_free, y_full, y_free = sem("x_full"), sem("x_free"), sem("y_full"), sem("y_free")
        sv_s, less_s, dist_s, exp_s, sign_s, stdp_s, xb_s = (sem(n) for n in ("sv_s", "less_s", "dist_s", "exp_s", "sign_s", "stdp_s", "xb_s"))
        gate_s, rt_hi_s = sem("gate_s"), sem("rt_hi_s")
        u_full, u_sb, u_lo_s, v_full, v_sb = sem("u_full"), sem("u_sb"), sem("u_lo_s"), sem("v_full"), sem("v_sb")
        s_full, s_masked, p_exp, p_inv, p_norm = sem("s_full"), sem("s_masked"), sem("p_exp"), sem("p_inv"), sem("p_norm")
        pt_full, pt_sb, pv_done, o_sb = sem("pt_full"), sem("pt_sb"), sem("pv_done"), sem("o_sb")
        stored = sem("stored")

        LAST = PAIRS * STEPS

        def heads_at(n):
            if n < 0:
                return [0, 1]
            h = (n + U_AHEAD) // 2
            return [h] if (n + U_AHEAD) % 2 == 0 and 2 <= h < PAIRS * H else []

        def chunks_at(n):
            if n < 0:
                return [0, 1]
            c = (n + V_AHEAD) // 2
            return [c] if (n + V_AHEAD) % 2 == 0 and 2 <= c < PAIRS * CH else []

        def v_bank(c):
            return s_ps[1] if c == 1 else v_ps

        def walk(side, main):
            at = Tally()
            for job, t0, nt in PROLOGUE:
                side(job, t0, nt, at)
                at.passed(job, t0, nt)
            for n in range(-1, LAST + PV_LAG):
                main(n, at)
                p, step = divmod(n, STEPS)
                for job, off in BODY.get(step, []) if n >= 0 else []:
                    if 0 <= p + off < PAIRS and p < PAIRS:
                        side(job, (p + off) * TILES, TILES, at)
                        at.passed(job, (p + off) * TILES, TILES)
            for job, t0, nt in EPILOGUE:
                side(job, t0, nt, at)
                at.passed(job, t0, nt)

        block = ctx.enter_context(nc.Block())

        @block.sync
        def _(sp):
            sp.dma_start(x[:, 0:2, :], x_view[:, 0:2, :]).then_inc(ld_x0, 16)
            for dst, src in ((ga, ga_d), (wa, wa_d)):
                sp.dma_start(dst[:], src).then_inc(ld_a, 16)
            sp.dma_start(x[:, 2:TILES, :], x_view[:, 2:TILES, :]).then_inc(ld_x1, 16)
            for dst, src in ((woa, woa_d), (boa, boa_d)):
                sp.dma_start(dst[:], src).then_inc(ld_o, 16)
            for dst, src in ((wg_i, wg_d), (wu_i, wu_d), (wd_i, wd_d)):
                sp.dma_start(dst[:], src).then_inc(ld_f, 16)
            sp.dma_start(wk[:], wk_d).then_inc(ld_q, 16)
            sp.wait_ge(zeros_q, 2)
            for i in range(2):
                half = slice(i * A, (i + 1) * A)
                sp.dma_start(wq1[half, :, i, :], wq_d[half, :, :]).then_inc(ld_q, 16)
                sp.dma_start(bq1[half, i, :], bq_d[half, :]).then_inc(ld_q, 16)
            sp.dma_start(bv[:], bv_d).then_inc(ld_q, 16)
            sp.dma_start(bo[:], bo_d).then_inc(ld_q, 16)
            for p in range(1, PAIRS):
                sp.dma_start(x[:, p * TILES:(p + 1) * TILES, :], x_view[:, p * TILES:(p + 1) * TILES, :]).then_inc(ld_x, 16)

            def side(job, t0, nt, at):
                o, ts = t0 % TILES, bass.ds(t0, nt)
                tiles, cols = range(o, o + nt), slice(o * P, (o + nt) * P)
                if job == "down" and t0 in at.second:
                    sp.wait_ge(x_free, at.x + 1)
                    sp.dma_start(out_view[:, ts, :], x[:, ts, :]).then_inc(stored, 16)

            walk(side, lambda n, at: None)
            sp.wait_ge(stored, 16 * (PAIRS + 1))

        @block.tensor
        def _(pe):
            def split3(out, w_hi_ap, w_lo_ap, r_hi_ap, r_lo_ap):
                nc.tensor.matmul(out, w_hi_ap, r_hi_ap, start=True, stop=False)
                nc.tensor.matmul(out, w_lo_ap, r_hi_ap, start=False, stop=False)
                return nc.tensor.matmul(out, w_hi_ap, r_lo_ap, start=False, stop=True)

            def use_x(at):
                if at.x == 0:
                    return
                pe.wait_ge(x_free, at.x)

            def use_y(at):
                if at.y == 0:
                    return
                pe.wait_ge(y_free, at.y)

            def side(job, t0, nt, at):
                o, ts = t0 % TILES, bass.ds(t0, nt)
                tiles, cols = range(o, o + nt), slice(o * P, (o + nt) * P)
                if job in ("lntA", "lntF", "lntB"):
                    if at.n("lnt") == 0:
                        pe.wait_ge(consts, 1)
                    pe.wait_ge(xn_ready, at.after("lns1", t0, nt).n)
                    use_x(at)
                    for j in tiles:
                        last = nc.tensor.transpose(X[:, j * P:(j + 1) * P], xn[:, j, :], ident[:])
                    last.then_inc(x_full, 1)
                elif job.startswith("qkv"):
                    w = int(job[3])
                    if w == 0:
                        pe.wait_ge(wa_ready, 1)
                        pe.wait_ge(x_free, at.after("lnt", t0, nt).x)
                    if w == 1:
                        use_x(at)
                        split3(X[:, cols], wa_hi[:, w, :], wa_lo[:, w, :], xt_hi[:, cols], xt_lo[:, cols]).then_inc(x_full, 1)
                    else:
                        use_y(at)
                        split3(Y[:, cols], wa_hi[:, w, :], wa_lo[:, w, :], xt_hi[:, cols], xt_lo[:, cols]).then_inc(y_full, 1)
                elif job == "mean":
                    use_x(at)
                    use_y(at)
                    nc.tensor.matmul(X[:, cols], mean_w[:], t_qkv[:, 0, cols], start=True, stop=True).then_inc(x_full, 1)
                    for j in tiles:
                        last = nc.tensor.matmul(Y[:, j:j + 1], t_qkv[:, 1, j * P:(j + 1) * P], mean_w[:, 0:1], start=True, stop=True)
                    last.then_inc(y_full, 1)
                elif job == "vwo":
                    if at.n("vwo") == 0:
                        pe.wait_ge(ld_o, 32)
                    pe.wait_ge(sv_s, at.n("vwo") + 1)
                    use_x(at)
                    for j in tiles:
                        last = nc.tensor.matmul(X[:, j * D:(j + 1) * D], sv[:, j * P:(j + 1) * P], woa[:], start=True, stop=True)
                    last.then_inc(x_full, 1)
                elif job == "aout":
                    pe.wait_ge(x_free, at.after("vwo", t0, nt).x)
                    pe.wait_ge(stdp_s, at.n("aout") + 1)
                    use_y(at)
                    for q in tiles:
                        b, qt = divmod(q, 2)
                        for kt in range(2):
                            last = nc.tensor.matmul(Y[:, q * D:(q + 1) * D], stdp[:, 2 * b + kt, qt * P:(qt + 1) * P],
                                                    vwo[:, 2 * b + kt, :], start=(kt == 0), stop=(kt == 1))
                    last.then_inc(y_full, 1)
                elif job.startswith("gu"):
                    c = int(job[2])
                    if c == 0:
                        pe.wait_ge(wf_ready, 1)
                        pe.wait_ge(x_free, at.after("lnt", t0, nt).x)
                    cs = slice(c * P, (c + 1) * P)
                    use_x(at)
                    nc.tensor.matmul(X[:, cols], wg[:, cs], xt_hi[:, cols], start=True, stop=False)
                    nc.tensor.matmul(X[:, cols], wg[:, cs], xt_lo[:, cols], start=False, stop=True).then_inc(x_full, 1)
                    use_y(at)
                    nc.tensor.matmul(Y[:, cols], wu[:, cs], xt_hi[:, cols], start=True, stop=False)
                    nc.tensor.matmul(Y[:, cols], wu[:, cs], xt_lo[:, cols], start=False, stop=True).then_inc(y_full, 1)
                elif job == "down":
                    pe.wait_ge(y_free, at.after("gu", t0, nt).y)
                    use_x(at)
                    for j in tiles:
                        for c in range(FC):
                            last = nc.tensor.matmul(X[:, j * D:(j + 1) * D], hid[:, c, j * P:(j + 1) * P], wd[:, c, :],
                                                    start=(c == 0), stop=(c == FC - 1))
                    last.then_inc(x_full, 1)
                elif job == "bout":
                    pe.wait_ge(o_sb, at.n("bout") + 1)
                    use_x(at)
                    for j in tiles:
                        last = nc.tensor.transpose(X[:, j * P:(j + 1) * P], o_t[:, j * P:(j + 1) * P], ident[:])
                    last.then_inc(x_full, 1)
                elif job == "wb":
                    pe.wait_ge(w_lo, 8)
                    for i in range(H // 2):
                        nc.tensor.matmul(v_ps[:, 2 * i:2 * i + 2], wk[:, i, :], bq1[:, :, i], start=True, stop=True)
                    for i in range(H // 2):
                        last = nc.tensor.matmul(v_ps[:, H:H + 1], wo[:, i, :], bv[:, i:i + 1], start=(i == 0), stop=(i == H // 2 - 1))
                    last.then_inc(w_full, 1)
                elif job in WEIGHTS:
                    i = int(job[1])
                    if i == 0:
                        pe.wait_ge(ld_v, 16 * 3)
                    if i == 4:
                        pe.wait_ge(ld_q, 16 * 7)
                    if i >= 2:
                        pe.wait_ge(w_lo, i - 1)
                    left, right = (wv1, wo) if i < 4 else (wq1, wk)
                    for j in range(4):
                        h = 4 * (i % 4) + j
                        last = nc.tensor.matmul((u_ps, v_ps)[i % 2][:, j * D:(j + 1) * D], left[:, h // 2, h % 2, :], right[:, h // 2, :], start=True, stop=True)
                    last.then_inc(w_full, 1)

            def rows_ready(p, at):
                pe.wait_ge(rt_hi_s, at.n("lntB"))
                pe.wait_ge(x_free, at.after("lntB", p * TILES, TILES).x)

            def u_proj(h, at):
                p, i = divmod(h, H)
                if i == 0:
                    rows_ready(p, at)
                if h:
                    pe.wait_ge(u_lo_s, h)
                split3(u_ps[:], m_hi[:, i, :], m_lo[:, i, :], rt_hi[:, p % 2, :], rt_lo[:, p % 2, :]).then_inc(u_full, 1)

            def v_proj(c, at):
                p, i = divmod(c, CH)
                g, j = divmod(i, TILES)
                if i == 0:
                    rows_ready(p, at)
                if c > 1:
                    pe.wait_ge(v_sb, c if c > 2 else 1)
                hs = slice(GH * g, GH * (g + 1))
                js = slice(j * P, (j + 1) * P)
                split3(v_bank(c)[:], rt_hi[:, p % 2, js], rt_lo[:, p % 2, js], wvo_hi[:, hs, :], wvo_lo[:, hs, :]).then_inc(v_full, 1)

            def scores(n):
                p, step = divmod(n, STEPS)
                pe.wait_ge(u_lo_s, n // 2 + 1)
                if n == 1:
                    pe.wait_ge(v_sb, 2)
                elif n > 1:
                    pe.wait_ge(s_masked, n - 1)
                S, i, b, q = s_ps[n % 2], (n // 2) % 2, step % 2, p % 2
                t = b * N
                nc.tensor.matmul(S[:, 0:P], u[:, i, b, :], rt[:, q, t:t + P], start=True, stop=True)
                split3(S[:, P:SC], u_hi[:, i, b, :], u_lo[:, i, b, :], rt_hi[:, q, t:t + N], rt_lo[:, q, t:t + N]).then_inc(s_full, 1)

            def transposes(n):
                k = n - T_LAG
                pe.wait_ge(p_norm, k + 1)
                if k:
                    pe.wait_ge(pt_sb, k)
                for j in range(3):
                    last = nc.tensor.transpose(pt_ps[:, j * P:(j + 1) * P], prob[:, k % 4, j * P:(j + 1) * P], ident[:])
                last.then_inc(pt_full, 1)

            def weighted_sum(n):
                k = n - PV_LAG
                p, step = divmod(k, STEPS)
                h, b = divmod(step, 2)
                group = k // (2 * GH)
                pe.wait_ge(pt_sb, k + 1)
                pe.wait_ge(v_sb, TILES * (group + 1))
                if step == 0 and p:
                    pe.wait_ge(o_sb, p)
                hs = slice((h % GH) * D, (h % GH + 1) * D)
                vg = v[:, group % 2]
                nc.tensor.matmul(o_ps[:, b * N:(b + 1) * N], vg[:, 2 * b, hs], prob_t[:, k % 2, 0:N],
                                 start=(step == 0), stop=False, skip_group_check=True)
                nc.tensor.matmul(o_ps[:, b * N + P:(b + 1) * N], vg[:, 2 * b + 1, hs], prob_t[:, k % 2, N:SC],
                                 start=False, stop=(step >= STEPS - 2), skip_group_check=True).then_inc(pv_done, 1)

            def main(n, at):
                if n == -1:
                    pe.wait_ge(w_hi, 9)
                    pe.wait_ge(w_lo, 8)
                    u_proj(0, at)
                    v_proj(0, at)
                    v_proj(1, at)
                    u_proj(1, at)
                    return
                if n < LAST:
                    scores(n)
                for h in heads_at(n):
                    u_proj(h, at)
                if T_LAG <= n < LAST + T_LAG:
                    transposes(n)
                for c in chunks_at(n):
                    v_proj(c, at)
                if PV_LAG <= n < LAST + PV_LAG:
                    weighted_sum(n)

            walk(side, main)

        @block.scalar
        def _(act):
            act.dma_start(wo[:], wo_d).then_inc(ld_v, 16)
            act.wait_ge(consts_in, 4)
            nc.scalar.activation(warm[:], minus_half[:, 0:1], ACT.Tanh)
            act.wait_ge(zeros_v, 1)
            for i in range(2):
                half = slice(i * A, (i + 1) * A)
                act.dma_start(wv1[half, :, i, :], wv_d[half, :, :]).then_inc(ld_v, 16)

            def side(job, t0, nt, at):
                o, ts = t0 % TILES, bass.ds(t0, nt)
                tiles, cols = range(o, o + nt), slice(o * P, (o + nt) * P)
                if job in ("lntA", "lntF"):
                    act.wait_ge(x_full, at.x + 1)
                    if at.after("xt_read", t0, nt):
                        act.wait_ge(y_full, at.after("xt_read", t0, nt).y)
                    nc.scalar.activation(xt_hi[:, cols], X[:, cols], ACT.Copy).then_inc(xt_hi_s, 1)
                elif job == "lntB":
                    p = t0 // TILES
                    act.wait_ge(x_full, at.x + 1)
                    if p >= 2:
                        act.wait_ge(u_full, H * (p - 1))
                        act.wait_ge(v_full, CH * (p - 1))
                        act.wait_ge(s_full, STEPS * (p - 1))
                    nc.scalar.activation(rt[:, p % 2, cols], X[:, cols], ACT.Copy)
                    nc.scalar.activation(rt_hi[:, p % 2, cols], X[:, cols], ACT.Copy).then_inc(rt_hi_s, 1)
                elif job.startswith("qkv"):
                    w = int(job[3])
                    if at.n("qkv0") == 0:
                        act.wait_ge(ga_ready, 1)
                    if w == 1:
                        act.wait_ge(x_full, at.x + 1)
                        nc.scalar.activation(t_qkv[:, w, cols], X[:, cols], ACT.Tanh, bias=ga_bias[:, w:w + 1],
                                             scale=ga_scale[:, w:w + 1]).then_inc(x_free, 1)
                    else:
                        act.wait_ge(y_full, at.y + 1)
                        if w == 2 and at.n("qkv2"):
                            act.wait_ge(sv_s, at.n("qkv2"))
                        nc.scalar.activation(t_qkv[:, w, cols], Y[:, cols], ACT.Tanh, bias=ga_bias[:, w:w + 1],
                                             scale=ga_scale[:, w:w + 1]).then_inc(y_free, 1)
                elif job == "vwo":
                    act.wait_ge(x_full, at.x + 1)
                    nc.scalar.activation(vwo[:, o:o + nt, :], X[:, cols].rearrange("p (j d) -> p j d", d=D), ACT.Copy).then_inc(x_free, 1)
                elif job == "mat0":
                    act.wait_ge(x_free, at.after("mean", t0, nt).x)
                    act.wait_ge(y_free, at.after("mean", t0, nt).y)
                    for j in tiles:
                        b = j // 2
                        last = nc.scalar.activation(dist[:, j, :], tq[:, b * N:(b + 1) * N], ACT.Abs, bias=ntk[:, j:j + 1])
                    last.then_inc(dist_s, 1)
                    act.wait_ge(dist_s, at.n("mat0") + 1)
                    nc.scalar.activation(expd[:, o:o + nt, :], dist[:, o:o + nt, :], ACT.Exp, scale=-INV_TAU).then_inc(exp_s, 1)
                elif job.startswith("gu"):
                    act.wait_ge(x_full, at.x + 1)
                    if at.x:
                        act.wait_ge(x_free, at.x)
                    nc.scalar.activation(gate_t[:, cols], X[:, cols], ACT.Tanh, scale=0.5 * W_SCALE).then_inc(gate_s, 1)
                elif job == "wb":
                    act.wait_ge(w_full, 9)
                    nc.scalar.activation(u_bias[:], v_ps[:, 0:H], ACT.Copy, scale=SCORE_SCALE)
                    nc.scalar.activation(o_bias[:], v_ps[:, H:H + 1], ACT.Identity, bias=bo[:]).then_inc(w_hi, 1)
                elif job in WEIGHTS:
                    i = int(job[1])
                    act.wait_ge(w_full, i + 1)
                    dst = (wvo_hi, m_hi)[i // 4][:, 4 * (i % 4):4 * (i % 4) + 4, :]
                    nc.scalar.activation(dst, (u_ps, v_ps)[i % 2][:].rearrange("p (j d) -> p j d", d=D), ACT.Copy,
                                         scale=(1.0, SCORE_SCALE)[i // 4]).then_inc(w_hi, 1)

            def u_evac(h):
                act.wait_ge(u_full, h + 1)
                if h >= 2:
                    act.wait_ge(s_full, 2 * (h - 1))
                nc.scalar.activation(u[:, h % 2, :, :], u_tiles[:, :, 0, :], ACT.Identity, bias=u_bias[:, h % H:h % H + 1])
                nc.scalar.activation(u_hi[:, h % 2, :, :], u_tiles[:, :, 1, :], ACT.Identity, bias=u_bias[:, h % H:h % H + 1]).then_inc(u_sb, 1)

            def v_evac(c):
                g, j = divmod(c, TILES)
                act.wait_ge(v_full, c + 1)
                if g >= 2:
                    act.wait_ge(pv_done, 2 * GH * (g - 1))
                nc.scalar.activation(v[:, g % 2, j, :], v_bank(c)[:], ACT.Copy).then_inc(v_sb, 1)

            def exp(n):
                act.wait_ge(s_masked, n + 1)
                if n >= 4:
                    act.wait_ge(pt_full, n - 3)
                    act.wait_ge(p_inv, n - 3)
                q, r = n % 4, n % 2
                nc.scalar.activation(prob[:, q, 0:P], neg_s[:, r, 0:P], ACT.Exp, bias=neg_max[:, q, 0:1], scale=-1.0,
                                     accum_out=row_sum[:, q, 0:1])
                nc.scalar.activation(prob[:, q, P:SC], neg_s[:, r, P:SC], ACT.Exp, bias=neg_max[:, q, 1:2], scale=-1.0,
                                     accum_out=row_sum[:, q, 1:2]).then_inc(p_exp, 1)

            def pt_evac(n):
                k = n - T_LAG
                act.wait_ge(pt_full, k + 1)
                if k >= 2:
                    act.wait_ge(pv_done, k - 1)
                nc.scalar.activation(prob_t[:, k % 2, :], pt_ps[:, 0:SC], ACT.Copy).then_inc(pt_sb, 1)

            def main(n, at):
                if n == -1:
                    u_evac(0)
                    v_evac(0)
                    v_evac(1)
                    u_evac(1)
                    return
                for h in heads_at(n):
                    u_evac(h)
                if T_LAG <= n < LAST + T_LAG:
                    pt_evac(n)
                for c in chunks_at(n):
                    v_evac(c)
                if n < LAST:
                    exp(n)
                k = n - PV_LAG
                if k < 0 or k % STEPS < STEPS - 1:
                    return
                act.wait_ge(pv_done, k + 1)
                if k >= STEPS:
                    act.wait_ge(x_full, at.after("bout", 0, TILES).x)
                for cols in [slice(0, N), slice(N, PAIR)] if k == LAST - 1 else [slice(0, PAIR)]:
                    nc.scalar.activation(o_t[:, cols], o_ps[:, cols], ACT.Identity, bias=o_bias[:]).then_inc(o_sb, 1)

            walk(side, main)

        @block.vector
        def _(dve):
            nc.vector.memset(wv1[:], 0.0).then_inc(zeros_v, 1)

            def link(ins, at):
                ins.then_inc(link_s, 1)
                at.link += 1
                dve.wait_ge(link_s, at.link)

            def side(job, t0, nt, at):
                o, ts = t0 % TILES, bass.ds(t0, nt)
                tiles, cols = range(o, o + nt), slice(o * P, (o + nt) * P)
                if job == "lns0":
                    if t0 in at.added:
                        dve.wait_ge(x_free, at.after("add", t0, nt).x)
                        dve.wait_ge(y_free, at.after("add", t0, nt).y)
                    elif t0 >= TILES:
                        dve.wait_ge(ld_x, 16 * (PAIRS - 1))
                    else:
                        dve.wait_ge(ld_x1 if t0 else ld_x0, 16)
                    for j in tiles:
                        last = nc.vector.bn_stats(stats[:, j, :], x[:, t0 - o + j, :])
                    link(last, at)
                    for j in tiles:
                        last = nc.vector.bn_aggr(mv[:, j, :], stats[:, j, :])
                    link(last, at)
                    nc.vector.tensor_scalar(var[:, o:o + nt], mv[:, o:o + nt, 1], EPS, None, ALU.add).then_inc(ln_var, 1)
                elif job == "lns1":
                    dve.wait_ge(ln_rstd, at.after("lns0", t0, nt).n)
                    if at.after("lnt", t0, nt):
                        dve.wait_ge(x_full, at.after("lnt", t0, nt).x)
                    for j in tiles:
                        last = nc.vector.tensor_scalar(xn[:, j, :], x[:, t0 - o + j, :], mv[:, j, 0:1], rstd[:, j:j + 1], ALU.subtract, ALU.mult)
                    last.then_inc(xn_ready, 1)
                    if at.n("lns1") == 0:
                        dve.wait_ge(ld_a, 32)
                        link(nc.vector.tensor_copy(wa_hi[:], wa[:]), at)
                        nc.vector.tensor_tensor(wa_lo[:], wa[:], wa_hi[:].bitcast(F32), ALU.subtract).then_inc(wa_ready, 1)
                        nc.vector.tensor_scalar(ga_tmp[:], ga[:, 3, :], EPS, None, ALU.add).then_inc(ga_v, 1)
                        dve.wait_ge(ga_pow, 1)
                        link(nc.vector.scalar_tensor_tensor(ga_scale[:], ga_rs[:], 2.0, ga[:, 0, :], ALU.mult, ALU.mult), at)
                        link(nc.vector.tensor_tensor(ga_tmp[:], ga[:, 2, :], ga_scale[:], ALU.mult), at)
                        link(nc.vector.scalar_tensor_tensor(ga_bias[:], ga[:, 1, :], 2.0, ga_tmp[:], ALU.mult, ALU.subtract), at)
                        nc.vector.tensor_scalar(ga_bias[:], ga_bias[:], -2.0, None, ALU.add).then_inc(ga_ready, 1)
                elif job in ("lntA", "lntF"):
                    dve.wait_ge(xt_hi_s, at.n("xt") + 1)
                    nc.vector.tensor_tensor(xt_lo[:, cols], X[:, cols], xt_hi[:, cols].bitcast(F32), ALU.subtract).then_inc(x_free, 1)
                elif job == "lntB":
                    q = t0 // TILES % 2
                    dve.wait_ge(rt_hi_s, at.n("lntB") + 1)
                    nc.vector.tensor_tensor(rt_lo[:, q, cols], X[:, cols], rt_hi[:, q, cols].bitcast(F32), ALU.subtract).then_inc(x_free, 1)
                elif job == "qkv2":
                    if at.n("qkv2") == 0:
                        dve.wait_ge(ld_f, 48)
                        nc.vector.tensor_copy(wg[:], wg_i[:])
                        nc.vector.tensor_copy(wu[:], wu_i[:])
                        nc.vector.tensor_copy(wd[:], wd_i[:]).then_inc(wf_ready, 1)
                elif job == "mean":
                    dve.wait_ge(x_full, at.x + 1)
                    nc.vector.tensor_scalar(tq[:, cols], X[:, cols], 0.5, None, ALU.add).then_inc(x_free, 1)
                    dve.wait_ge(y_full, at.y + 1)
                    nc.vector.tensor_scalar(ntk[:, o:o + nt], Y[:, o:o + nt], 0.5, -1.0, ALU.add, ALU.mult).then_inc(y_free, 1)
                elif job == "mat0":
                    dve.wait_ge(x_free, at.after("mean", t0, nt).x)
                    dve.wait_ge(y_free, at.after("mean", t0, nt).y)
                    for j in tiles:
                        b = j // 2
                        last = nc.vector.tensor_scalar(less[:, j, :], tq[:, b * N:(b + 1) * N], ntk[:, j:j + 1], 0.0, ALU.add, ALU.is_lt)
                    last.then_inc(less_s, 1)
                elif job == "mat1":
                    dve.wait_ge(less_s, at.n("mat1") + 1)
                    dve.wait_ge(exp_s, at.n("mat1") + 1)
                    nc.vector.scalar_tensor_tensor(signed[:, o:o + nt, :], less[:, o:o + nt, :], -0.5, expd[:, o:o + nt, :],
                                                   ALU.add, ALU.mult).then_inc(sign_s, 1)
                elif job == "aout":
                    dve.wait_ge(y_full, at.y + 1)
                    dve.wait_ge(xb_s, at.n("aout") + 1)
                    nc.vector.tensor_tensor(x[:, ts, :], Y[:, cols].rearrange("p (j d) -> p j d", d=D), xb[:, o:o + nt, :], ALU.add).then_inc(y_free, 1)
                elif job.startswith("gu"):
                    c = int(job[2])
                    dve.wait_ge(gate_s, at.n("gu") + 1)
                    if at.y:
                        dve.wait_ge(y_free, at.y)
                    nc.vector.scalar_tensor_tensor(gated[:, cols], gate_t[:, cols], 1.0, X[:, cols], ALU.add, ALU.mult).then_inc(x_free, 1)
                    dve.wait_ge(x_free, at.x + 1)
                    dve.wait_ge(y_full, at.y + 1)
                    nc.vector.tensor_tensor(hid[:, c, cols], gated[:, cols], Y[:, cols], ALU.mult).then_inc(y_free, 1)
                elif job == "down":
                    dve.wait_ge(x_full, at.x + 1)
                    xs = x[:, ts, :]
                    nc.vector.scalar_tensor_tensor(xs, X[:, cols].rearrange("p (j d) -> p j d", d=D), 0.5 * W_SCALE ** 3, xs,
                                                   ALU.mult, ALU.add).then_inc(x_free, 1)
                elif job == "bout":
                    dve.wait_ge(x_full, at.x + 1)
                    xs = x[:, ts, :]
                    nc.vector.tensor_tensor(xs, X[:, cols].rearrange("p (j d) -> p j d", d=D), xs, ALU.add).then_inc(x_free, 1)
                elif job == "wb":
                    pass
                elif job in WEIGHTS:
                    i = int(job[1])
                    dve.wait_ge(w_hi, i + 1)
                    hs = slice(4 * (i % 4), 4 * (i % 4) + 4)
                    hi, lo = ((wvo_hi, wvo_lo), (m_hi, m_lo))[i // 4]
                    nc.vector.scalar_tensor_tensor(lo[:, hs, :], (u_ps, v_ps)[i % 2][:].rearrange("p (j d) -> p j d", d=D),
                                                   (1.0, SCORE_SCALE)[i // 4], hi[:, hs, :].bitcast(F32), ALU.mult, ALU.subtract).then_inc(w_lo, 1)

            def u_low(h):
                dve.wait_ge(u_sb, h + 1)
                nc.vector.scalar_tensor_tensor(u_lo[:, h % 2, :, :], u_tiles[:, :, 1, :], u_bias[:, h % H:h % H + 1],
                                               u_hi[:, h % 2, :, :].bitcast(F32), ALU.add, ALU.subtract).then_inc(u_lo_s, 1)

            def main(n, at):
                if n == 0:
                    dve.wait_ge(consts, 2)
                if 0 <= n < LAST:
                    dve.wait_ge(s_full, n + 1)
                    if n >= 2:
                        dve.wait_ge(p_exp, n - 1)
                    r, q = n % 2, n % 4
                    nc.vector.tensor_tensor_reduce(out=neg_s[:, r, 0:P], in0=s_ps[r][:, 0:P], in1=mask[:, P:N], scale=-1.0, scalar=3e38,
                                                   op0=ALU.add, op1=ALU.min, accum_out=neg_max[:, q, 0:1])
                    nc.vector.tensor_tensor_reduce(out=neg_s[:, r, P:SC], in0=s_ps[r][:, P:SC], in1=mask[:], scale=-1.0, scalar=3e38,
                                                   op0=ALU.add, op1=ALU.min, accum_out=neg_max[:, q, 1:2]).then_inc(s_masked, 1)
                if 1 <= n < LAST + 1:
                    k = n - 1
                    q = k % 4
                    dve.wait_ge(p_exp, k + 1)
                    nc.vector.reciprocal(row_inv[:, q, :], row_sum[:, q, :]).then_inc(p_inv, 1)
                    dve.wait_ge(p_inv, k + 1)
                    nc.vector.tensor_scalar(prob[:, q, 0:P], prob[:, q, 0:P], row_inv[:, q, 0:1], None, ALU.mult)
                    nc.vector.tensor_scalar(prob[:, q, P:SC], prob[:, q, P:SC], row_inv[:, q, 1:2], None, ALU.mult).then_inc(p_norm, 1)
                for h in heads_at(n):
                    u_low(h)

            walk(side, main)

        @block.gpsimd
        def _(pool):
            nc.gpsimd.memset(ident[:], 0.0).then_inc(consts_in, 1)
            nc.gpsimd.memset(mask[:], 0.0).then_inc(consts_in, 1)
            nc.gpsimd.memset(mean_w[:], -0.5 / D).then_inc(consts_in, 1)
            nc.gpsimd.memset(minus_half[:], -0.5).then_inc(consts_in, 1)
            nc.gpsimd.memset(bq1[:], 0.0).then_inc(zeros_q, 1)
            nc.gpsimd.memset(wq1[:], 0.0).then_inc(zeros_q, 1)
            pool.wait_ge(consts_in, 4)
            nc.gpsimd.affine_select(out=ident[:], in_=ident[:], compare_op=ALU.not_equal, fill=1.0, base=0,
                                    pattern=[[-1, P]], channel_multiplier=1).then_inc(consts, 1)
            nc.gpsimd.affine_select(out=mask[:, P:N], in_=mask[:, P:N], compare_op=ALU.is_ge, fill=-BIG, base=0,
                                    pattern=[[-1, P]], channel_multiplier=1).then_inc(consts, 1)

            def side(job, t0, nt, at):
                o, ts = t0 % TILES, bass.ds(t0, nt)
                tiles, cols = range(o, o + nt), slice(o * P, (o + nt) * P)
                if job == "lns0":
                    pool.wait_ge(ln_var, at.n("lns0") + 1)
                    nc.gpsimd.tensor_tensor(rstd[:, o:o + nt], var[:, o:o + nt], minus_half[:, 0:nt], ALU.pow).then_inc(ln_rstd, 1)
                elif job == "lns1" and at.n("lns1") == 0:
                    pool.wait_ge(ga_v, 1)
                    nc.gpsimd.tensor_tensor(ga_rs[:], ga_tmp[:], minus_half[:, 0:3], ALU.pow).then_inc(ga_pow, 1)
                elif job == "qkv2":
                    pool.wait_ge(y_free, at.y + 1)
                    nc.gpsimd.tensor_scalar(sv[:, cols], t_qkv[:, 2, cols], 0.5, 0.5, ALU.mult, ALU.add).then_inc(sv_s, 1)
                elif job == "mat0":
                    if at.n("mat0") == 0:
                        pool.wait_ge(ld_o, 32)
                    nc.gpsimd.tensor_tensor(xb[:, o:o + nt, :], x[:, ts, :], boa[:, :].unsqueeze(1).to_broadcast([P, nt, D]), ALU.add).then_inc(xb_s, 1)
                elif job == "mat1":
                    pool.wait_ge(sign_s, at.n("mat1") + 1)
                    nc.gpsimd.tensor_scalar(stdp[:, o:o + nt, :], signed[:, o:o + nt, :], 2.0 * A_STDP, W_OFF, ALU.mult, ALU.add).then_inc(stdp_s, 1)

            walk(side, lambda n, at: None)


def kernel(**inputs):
    import numpy as np
    import concourse.bacc as bacc
    from concourse.bass_utils import run_bass_kernel_spmd

    a = {k.removeprefix("L0_"): np.asarray(v) for k, v in inputs.items()}
    x = a["attn_a_x"]

    def head_pairs(w):
        return w.reshape(H // 2, P, D).transpose(1, 0, 2)

    arrays = {
        "x": x.reshape(B * N, D),
        "wa": np.stack([a[f"attn_a_W{c}"] for c in "qkv"], 1),
        "ga": np.stack([np.stack([a[f"attn_a_{n}{c}"] for c in "qkv"], 1) for n in "gbmv"], 1),
        "woa": a["attn_a_Wo"],
        "boa": np.tile(a["attn_a_bo"][None, :], (P, 1)),
        "wq": head_pairs(a["attn_b_Wq"].transpose(0, 2, 1)),
        "wk": head_pairs(a["attn_b_Wk"].transpose(0, 2, 1)),
        "wv": head_pairs(a["attn_b_Wv"].transpose(0, 2, 1)),
        "wo": head_pairs(a["attn_b_Wo"]),
        "bq": a["attn_b_bq"].reshape(H // 2, P).T,
        "bv": a["attn_b_bv"].reshape(H // 2, P).T,
        "bo": a["attn_b_bo"][:, None],
        "wg": a["ffn_w_gate"].T,
        "wu": a["ffn_w_up"].T,
        "wd": a["ffn_w_down"].T.reshape(FC, P, D).transpose(1, 0, 2),
    }
    arrays = {f"{k}_in": np.ascontiguousarray(v) for k, v in arrays.items()}
    nc = bacc.Bacc("TRN2", target_bir_lowering=False, num_devices=1)
    args = [nc.dram_tensor(k, v.shape, mybir.dt.from_np(v.dtype), kind="ExternalInput").ap() for k, v in arrays.items()]
    out = nc.dram_tensor("out", (B * N, D), F32, kind="ExternalOutput").ap()
    build(nc, *args, out)
    r = run_bass_kernel_spmd(nc, [arrays], core_ids=[0])
    return r.results[0]["out"].reshape(x.shape)
```
